# Optimizing a Trainium2 kernel written in Bass

```python
import numpy as np
import jax
import jax.numpy as jnp

def _softmax(x, axis=-1):
    return jax.nn.softmax(x, axis=axis)

def _gelu(x):
    return jax.nn.gelu(x, approximate=True)

def _silu(x):
    return jax.nn.silu(x)

def _sigmoid(x):
    return jax.nn.sigmoid(x)

def _layernorm(x, axis=-1, eps=1e-05):
    m = jnp.mean(x, axis=axis, keepdims=True)
    v = jnp.var(x, axis=axis, keepdims=True)
    return (x - m) / jnp.sqrt(v + eps)

def _scatter_add(tgt, idx, src, axis=0):
    return tgt.at[idx].add(src)

def _segment_sum(src, seg, n):
    return jax.ops.segment_sum(src, seg, n)
kernel_name = 'mk_flamingo_gated_d1_seqx_r2_65f1e9'

def setup_inputs(seed: int=0):
    np.random.seed(seed)
    _w = jnp.asarray

    def _rec_inputs():
        import jax
        import jax.numpy as jnp
        _rk = jax.random.key(seed)
        x = -0.0002928 + 1 * jax.random.normal(jax.random.fold_in(_rk, 1), (8, 512, 512), jnp.float32)
        _lenS = 512 - jax.random.randint(jax.random.fold_in(_rk, 7), (8,), 0, max(1, 512 // 4) + 1, jnp.int32)
        _lenS2 = 512 - jax.random.randint(jax.random.fold_in(_rk, 8), (8,), 0, max(1, 512 // 4) + 1, jnp.int32)
        _ctx_1024P = jax.random.normal(jax.random.fold_in(_rk, 11), (8, 16, 512), jnp.float32)
        _ctx_1024c = jax.random.dirichlet(jax.random.fold_in(_rk, 511), 0.3 * jnp.ones((16,), jnp.float32), (8, 512))
        _ctx_1024t = jnp.einsum('bsk,bkd->bsd', _ctx_1024c, _ctx_1024P)
        _ctx_1024t = _ctx_1024t * jax.lax.rsqrt(jnp.mean(jnp.square(_ctx_1024t)) + 1e-12) * 0.953939
        ctx_1024 = -1.39393e-06 + 0.999914 * (_ctx_1024t + 0.3 * jax.random.normal(jax.random.fold_in(_rk, 611), (8, 512, 512), jnp.float32))
        _g = jax.random.normal(jax.random.fold_in(_rk, 9001), (2, 1), jnp.float32)
        _g = jnp.sign(_g) * jnp.maximum(jnp.abs(_g), 1.0) + (_g == 0) * 1.0
        g_xattn = _g[0]
        g_ffn = _g[1]
        return (x, ctx_1024, g_xattn, g_ffn)
    x, ctx_1024, g_xattn, g_ffn = _rec_inputs()

    def _L0_xattn_setup():
        import math
        import jax, jax.numpy as jnp
        import numpy as np
        B, S, H, NH = (2, 1024, 512, 4)
        DH = H // NH

        def _mlstm_parallel(qh, kh, vh, ig, fg, eps=1e-06):
            b, nh, s, dh = qh.shape
            log_f = jax.nn.log_sigmoid(fg)
            pcs = jnp.pad(jnp.cumsum(log_f, axis=-1), ((0, 0), (0, 0), (1, 0)))
            mat = pcs[..., :, None] - pcs[..., None, :]
            ltr = jnp.tril(jnp.ones((s, s), dtype=bool))
            log_fg_matrix = jnp.where(ltr, mat[..., 1:, 1:], -jnp.inf)
            log_D = log_fg_matrix + ig[..., None, :]
            max_log_D = jnp.max(log_D, axis=-1, keepdims=True)
            D = jnp.exp(log_D - max_log_D)
            qk = jnp.einsum('bhsd,bhtd->bhst', qh, kh) / math.sqrt(dh)
            C = qk * D
            normalizer = jnp.maximum(jnp.abs(C.sum(axis=-1, keepdims=True)), jnp.exp(-max_log_D))
            Cn = C / (normalizer + eps)
            return jnp.einsum('bhst,bhtd->bhsd', Cn, vh)
        key = jax.random.key(seed)
        ks = jax.random.split(key, 8)
        gate_std = 1.0 / math.sqrt(3 * H)
        return {'q': jax.random.normal(ks[0], (B, S, H), jnp.float32), 'k': jax.random.normal(ks[1], (B, S, H), jnp.float32), 'v': jax.random.normal(ks[2], (B, S, H), jnp.float32), 'w_igate': jax.random.normal(ks[3], (NH, 3 * H), jnp.float32) * gate_std, 'b_igate': jax.random.normal(ks[4], (NH,), jnp.float32) * 0.1, 'w_fgate': jax.random.normal(ks[5], (NH, 3 * H), jnp.float32) * gate_std, 'b_fgate': jnp.linspace(3.4, 6.0, NH, dtype=jnp.float32), 'ln_weight': jnp.zeros((H,), jnp.float32)}
    _L0_xattn_all = _L0_xattn_setup()
    _L0_xattn_in = {k: v for k, v in _L0_xattn_all.items() if k in ('w_igate', 'b_igate', 'w_fgate', 'b_fgate', 'ln_weight')}
    del _L0_xattn_all

    def _L0_ffn_setup():
        import jax, jax.numpy as jnp
        import numpy as np
        E = 8
        K = 2
        CAP_RATIO = 1.05
        key = jax.random.key(seed)
        ks = jax.random.split(key, 4)
        B, S, D, H = (2, 1024, 512, 2048)
        x = jax.random.normal(ks[0], (B, S, D), jnp.float32)
        Wg = jax.random.normal(ks[1], (E, D), jnp.float32) * 0.02
        W1 = jax.random.normal(ks[2], (E, D, H), jnp.float32) * 0.02
        b1 = jnp.zeros((E, H), jnp.float32)
        W2 = jax.random.normal(ks[3], (E, H, D), jnp.float32) * 0.02
        b2 = jnp.zeros((E, D), jnp.float32)
        return {'x': x, 'Wg': Wg, 'W1': W1, 'b1': b1, 'W2': W2, 'b2': b2}
    _L0_ffn_all = _L0_ffn_setup()
    _L0_ffn_in = {k: v for k, v in _L0_ffn_all.items() if k in ('Wg', 'W1', 'b1', 'W2', 'b2')}
    del _L0_ffn_all
    return {'x': x, 'ctx_1024': ctx_1024, 'g_xattn': g_xattn, 'g_ffn': g_ffn, 'L0_xattn_w_igate': _L0_xattn_in['w_igate'], 'L0_xattn_b_igate': _L0_xattn_in['b_igate'], 'L0_xattn_w_fgate': _L0_xattn_in['w_fgate'], 'L0_xattn_b_fgate': _L0_xattn_in['b_fgate'], 'L0_xattn_ln_weight': _L0_xattn_in['ln_weight'], 'L0_ffn_Wg': _L0_ffn_in['Wg'], 'L0_ffn_W1': _L0_ffn_in['W1'], 'L0_ffn_b1': _L0_ffn_in['b1'], 'L0_ffn_W2': _L0_ffn_in['W2'], 'L0_ffn_b2': _L0_ffn_in['b2']}

def reference(x, ctx_1024, g_xattn, g_ffn, L0_xattn_w_igate, L0_xattn_b_igate, L0_xattn_w_fgate, L0_xattn_b_fgate, L0_xattn_ln_weight, L0_ffn_Wg, L0_ffn_W1, L0_ffn_b1, L0_ffn_W2, L0_ffn_b2):
    import jax
    import jax.numpy as jnp

    def _L0_xattn_ref(q, k, v, w_igate, b_igate, w_fgate, b_fgate, ln_weight):
        import math
        import jax, jax.numpy as jnp
        import numpy as np
        B, S, H, NH = (2, 1024, 512, 4)
        DH = H // NH

        def _mlstm_parallel(qh, kh, vh, ig, fg, eps=1e-06):
            b, nh, s, dh = qh.shape
            log_f = jax.nn.log_sigmoid(fg)
            pcs = jnp.pad(jnp.cumsum(log_f, axis=-1), ((0, 0), (0, 0), (1, 0)))
            mat = pcs[..., :, None] - pcs[..., None, :]
            ltr = jnp.tril(jnp.ones((s, s), dtype=bool))
            log_fg_matrix = jnp.where(ltr, mat[..., 1:, 1:], -jnp.inf)
            log_D = log_fg_matrix + ig[..., None, :]
            max_log_D = jnp.max(log_D, axis=-1, keepdims=True)
            D = jnp.exp(log_D - max_log_D)
            qk = jnp.einsum('bhsd,bhtd->bhst', qh, kh) / math.sqrt(dh)
            C = qk * D
            normalizer = jnp.maximum(jnp.abs(C.sum(axis=-1, keepdims=True)), jnp.exp(-max_log_D))
            Cn = C / (normalizer + eps)
            return jnp.einsum('bhst,bhtd->bhsd', Cn, vh)
        b, s, h = q.shape
        nh = b_igate.shape[0]
        dh = h // nh
        gin = jnp.concatenate([q, k, v], axis=-1)
        ig = jnp.einsum('bsd,hd->bhs', gin, w_igate) + b_igate[None, :, None]
        fg = jnp.einsum('bsd,hd->bhs', gin, w_fgate) + b_fgate[None, :, None]
        qh = q.reshape(b, s, nh, dh).transpose(0, 2, 1, 3)
        kh = k.reshape(b, s, nh, dh).transpose(0, 2, 1, 3)
        vh = v.reshape(b, s, nh, dh).transpose(0, 2, 1, 3)
        hst = _mlstm_parallel(qh, kh, vh, ig, fg)
        mean = hst.mean(axis=-1, keepdims=True)
        var = hst.var(axis=-1, keepdims=True)
        hn = (hst - mean) / jnp.sqrt(var + 1e-05)
        scale = (1.0 + ln_weight).reshape(nh, dh)
        hn = hn * scale[None, :, None, :]
        return hn.transpose(0, 2, 1, 3).reshape(b, s, h)

    def _L0_ffn_ref(x, Wg, W1, b1, W2, b2):
        import jax, jax.numpy as jnp
        import numpy as np
        E = 8
        K = 2
        CAP_RATIO = 1.05
        B, S, D = x.shape
        T = B * S
        xf = x.reshape(T, D)
        gates = jax.nn.softmax(xf @ Wg.T, axis=-1)
        topw, topi = jax.lax.top_k(gates, K)
        C = int(round(K * T * CAP_RATIO / E))
        e_ord = topi.T.reshape(-1)
        tok_ord = jnp.tile(jnp.arange(T), K)
        oh = jax.nn.one_hot(e_ord, E, dtype=jnp.int32)
        cnt = jnp.take_along_axis(jnp.cumsum(oh, 0) - oh, e_ord[:, None], 1)[:, 0]
        within = cnt < C
        pos = jnp.where(within, cnt, C)
        x_disp = xf[tok_ord]
        buf = jnp.zeros((E, C + 1, D), xf.dtype).at[e_ord, pos].add(x_disp)[:, :C]
        h = jax.nn.gelu(jnp.einsum('ecd,edh->ech', buf, W1) + b1[:, None, :], approximate=False)
        y = jnp.einsum('ech,ehd->ecd', h, W2) + b2[:, None, :]
        y_ord = y[e_ord, jnp.minimum(pos, C - 1)] * within[:, None].astype(y.dtype)
        y_tk = y_ord.reshape(K, T, D).transpose(1, 0, 2)
        cw = topw * within.reshape(K, T).T.astype(topw.dtype)
        out = jnp.einsum('tk,tkd->td', cw, y_tk)
        return out.reshape(B, S, D)
    x = x + jnp.tanh(g_xattn[0]) * _L0_xattn_ref(_layernorm(x, axis=-1), ctx_1024, ctx_1024, L0_xattn_w_igate, L0_xattn_b_igate, L0_xattn_w_fgate, L0_xattn_b_fgate, L0_xattn_ln_weight)
    x = x + jnp.tanh(g_ffn[0]) * _L0_ffn_ref(_layernorm(x, axis=-1), L0_ffn_Wg, L0_ffn_W1, L0_ffn_b1, L0_ffn_W2, L0_ffn_b2)
    return x

_drawn_inputs = setup_inputs


def setup_inputs(seed=0):
    import zlib

    import numpy as np

    out = dict(_drawn_inputs(seed))
    spreads = {'L0_xattn_ln_weight': (0.0, 0.1), 'L0_ffn_b1': (0.0, 0.773), 'L0_ffn_b2': (0.0, 0.409)}
    factors = {'L0_xattn_b_igate': 64.0}
    for name, (base, spread) in spreads.items():
        noise = np.random.default_rng([zlib.crc32(name.encode()), seed]).standard_normal(out[name].shape)
        drawn = base * np.exp(spread * noise) if base else spread * noise
        out[name] = jnp.asarray(drawn.astype(out[name].dtype))
    for name, factor in factors.items():
        out[name] = (out[name] * factor).astype(out[name].dtype)
    return out
```

```python
from contextlib import ExitStack

import concourse.bass as bass
from concourse import mybir

F32 = mybir.dt.float32
F32R = mybir.dt.float32r
I32 = mybir.dt.int32
U32 = mybir.dt.uint32
ALU = mybir.AluOpType
ACT = mybir.ActivationFunctionType
AX = mybir.AxisListType

P = 128
B, S, D = 8, 512, 512
NH = 4
DH = D // NH
ST = S // P
KT = D // P
E = 8
HID = 2048
HT = HID // P
TOK = B * S
TT = TOK // P
TOPK = 2
CAP = int(round(TOPK * TOK * 1.05 / E))
HI = -(-CAP // P)
TAIL = CAP - (HI - 1) * P
PAD = P
NQ = TOPK * TT
LN_EPS = 1e-5
NORM_EPS = 1e-6
SCORE_SCALE = float(DH) ** -0.5
VW = DH + 2
GR = 36
DROPPED = 1000.0
LOWEST = -3.0e38


class Chain:

    def __init__(self, engine, signal, turn=0, per_turn=0):
        self.engine, self.sem, self.turn, self.per_turn, self.n = engine, signal, turn, per_turn, 0

    def __call__(self, ins):
        self.n += 1
        ins.then_inc(self.sem, 1)
        self.engine.wait_ge(self.sem, self.turn * self.per_turn + self.n)

    def closed(self):
        assert self.n == self.per_turn, (self.sem, self.n)


def build(nc, x, ctx_in, g_xattn, g_ffn, w_ig, b_ig, w_fg, b_fg, ln_w, w_router, w1, b1, w2, b2, out):
    x_rows = x.rearrange("b (t p) d -> b p t d", p=P)
    ctx_rows = ctx_in.rearrange("b (t p) (h c) -> b t p h c", p=P, h=NH)
    xn_dram = nc.dram_tensor("xn_rows", (TOK + PAD, D), F32, kind="Internal").ap()
    negmax_dram = nc.dram_tensor("negmax_rows", (B, NH * S), F32, kind="Internal").ap()
    out_rows = out[0:TOK, :].rearrange("(b t p) d -> b p t d", b=B, p=P)
    xn_rows = xn_dram[0:TOK, :].rearrange("(b t p) d -> b p t d", b=B, p=P)

    stack = ExitStack()
    with stack:
        def sb(name, shape, dt=F32, where=stack):
            return where.enter_context(nc.sbuf_tensor(name, shape, dt))

        def sem(name):
            return stack.enter_context(nc.semaphore(name))

        PS = stack.enter_context(nc.psum_tensor("PS", [P, 8, 512], F32))

        ident = sb("ident", [P, P])
        b1_all = sb("b1_all", [P, E * HT])
        slot_row = sb("slot_row", [P, E * HI], I32)
        slot_weight = sb("slot_weight", [P, E * HI])

        a_mem = ExitStack()
        ones = sb("ones", [P, S], F32, a_mem)
        zeros = sb("zeros", [P, D], F32, a_mem)
        logits = sb("logits", [P, TT, E], F32, a_mem)
        gate_bias = sb("gate_bias", [GR, 1], F32, a_mem)
        tanh_x = sb("tanh_x", [P, 1], F32, a_mem)
        wrouter = sb("wrouter", [P, KT, E], F32, a_mem)
        wgate = sb("wgate", [P, 2 * KT, GR], F32, a_mem)
        tanh_f = sb("tanh_f", [P, 1], F32, a_mem)
        xs = [sb(f"xs{p}", [P, ST, D], F32, a_mem) for p in range(2)]
        vs = [sb(f"vs{p}", [P, ST, NH, VW], F32, a_mem) for p in range(2)]
        qn = sb("qn", [P, ST, D], F32, a_mem)
        qT = [sb(f"qT{p}", [P, KT, S], F32, a_mem) for p in range(2)]
        kT = [sb(f"kT{p}", [P, KT, S], F32, a_mem) for p in range(2)]
        decay = [sb(f"decay{p}", [P, ST, S], F32, a_mem) for p in range(2)]
        negmax = [sb(f"negmax{p}", [P, NH, S], F32, a_mem) for p in range(2)]
        heads = sb("heads", [P, ST, NH, VW], F32, a_mem)
        xn = sb("xn", [P, ST, D], F32, a_mem)
        gvec = sb("gvec", [P, D], F32, a_mem)
        g_f = sb("g_f", [NH, S], F32, a_mem)
        g_i = sb("g_i", [NH, S], F32, a_mem)
        g_t = sb("g_t", [NH, S], F32, a_mem)
        g_cum = sb("g_cum", [NH, S], F32, a_mem)
        g_max = sb("g_max", [NH, S], F32, a_mem)
        g_rows = sb("g_rows", [GR, S], F32, a_mem)
        g_neg = sb("g_neg", [NH, S], F32, a_mem)
        cols = [sb(f"cols{p}", [P, ST, GR], F32, a_mem) for p in range(2)]
        expneg = [sb(f"expneg{p}", [P, ST, NH], F32, a_mem) for p in range(2)]
        st6 = sb("st6", [P, ST * NH, 6], F32, a_mem)
        sm = sb("sm", [P, 10, ST * NH], F32, a_mem)
        wload = sb("wload", [GR, 3 * D], F32, a_mem)
        rload = sb("rload", [E, D], F32, a_mem)
        bload = sb("bload", [E * HT, P], F32, a_mem)
        iota_e = sb("iota_e", [P, NQ, E], F32, a_mem)
        iota_p = sb("iota_p", [P, P], F32, a_mem)
        token = sb("token", [P, NQ], F32, a_mem)
        upper = sb("upper", [P, P], F32, a_mem)
        prob = sb("prob", [P, TT, E], F32, a_mem)
        work = sb("work", [P, NQ, E], F32, a_mem)
        chosen = sb("chosen", [P, NQ, E], F32, a_mem)
        base = sb("base", [P, NQ, E], F32, a_mem)
        rb = sb("rb", [P, 8, NQ], F32, a_mem)
        rb_i = sb("rb_i", [P, 3, NQ], I32, a_mem)
        one_lo = sb("one_lo", [P, 4, P], F32, a_mem)
        hi_vals = sb("hi_vals", [P, 4, 2, E * HI], F32, a_mem)
        pad_row = sb("pad_row", [P, 1], F32, a_mem)
        row_f = sb("row_f", [P, E * HI], F32, a_mem)
        a_mem.close()

        w_hi = sb("w_hi", [P, HT, 2 * D], F32R)
        w_lo = sb("w_lo", [P, HT, 2 * D], F32R)
        xa = [sb(f"xa{i}", [P, KT, 512], F32R) for i in range(2)]
        xb = [sb(f"xb{i}", [P, KT, 512], F32R) for i in range(2)]
        xt = [sb(f"xt{i}", [P, KT, TAIL + 1], F32R) for i in range(2)]
        h_raw = sb("h_raw", [P, 2, 512])
        h_hi = sb("h_hi", [P, 2, 512], F32R)
        h_lo = sb("h_lo", [P, 2, 512], F32R)
        y_out = sb("y_out", [P, 3, D])
        b2_row = sb("b2_row", [P, D])
        b1_now = sb("b1_now", [P, HT])
        weight_now = sb("weight_now", [P, HI])
        rows_now = sb("rows_now", [P, HI], I32)
        rows_next = sb("rows_next", [P, 4], I32)
        raw = sb("raw", [P, 2, 2, 2 * D])
        gathered = sb("gathered", [P, 3, D])

        const_in = sem("const_in")
        pool_const = sem("pool_const")
        weights_turned = sem("weights_turned")
        consts_ready = sem("consts_ready")
        tanh_made = sem("tanh_made")
        v_setup = sem("v_setup")
        batch_in = [sem(f"batch_in{p}") for p in range(2)]
        ln_var_made = sem("ln_var_made")
        ln_seed_made = sem("ln_seed_made")
        q_made = sem("q_made")
        turn_made = sem("turn_made")
        turn_copied = sem("turn_copied")
        gates_made = sem("gates_made")
        gates_taken = sem("gates_taken")
        abs_made = sem("abs_made")
        softplus_made = sem("softplus_made")
        negrow_made = sem("negrow_made")
        negrow_out = sem("negrow_out")
        negmax_in = [sem(f"negmax_in{p}") for p in range(2)]
        gate_rows_made = sem("gate_rows_made")
        cols_made = sem("cols_made")
        cols_copied = sem("cols_copied")
        expneg_made = sem("expneg_made")
        decay_made = sem("decay_made")
        decay_masked = sem("decay_masked")
        scores_made = sem("scores_made")
        scored = sem("scored")
        head_summed = sem("head_summed")
        head_copied = sem("head_copied")
        x1_made = sem("x1_made")
        xn_made = sem("xn_made")
        x1_stored = sem("x1_stored")
        xn_stored = sem("xn_stored")
        logits_made = sem("logits_made")
        logits_copied = sem("logits_copied")
        v_chain = sem("v_chain")
        a_chain = sem("a_chain")
        b_chain = sem("b_chain")
        b_sub = sem("b_sub")
        b_exp = sem("b_exp")
        choice_made = sem("choice_made")
        ranks_made = sem("ranks_made")
        onehot_made = sem("onehot_made")
        onehot_used = sem("onehot_used")
        table_summed = sem("table_summed")
        table_made = sem("table_made")
        raw_in = [sem(f"raw_in{i}") for i in range(2)]
        raw_used = sem("raw_used")
        w_ready = sem("w_ready")
        row_in = [sem(f"row_in{i}") for i in range(3)]
        rows_turned = sem("rows_turned")
        x_upper = sem("x_upper")
        x_ready = sem("x_ready")
        h_summed = sem("h_summed")
        h_made = sem("h_made")
        h_split = sem("h_split")
        y_step = sem("y_step")
        y_tile = sem("y_tile")
        y_taken = sem("y_taken")
        y_ready = sem("y_ready")
        y_added = sem("y_added")
        b2_in = sem("b2_in")
        rows_copied = sem("rows_copied")
        next_copied = sem("next_copied")
        b1_copied = sem("b1_copied")
        weight_copied = sem("weight_copied")

        V, A, G, T = nc.vector, nc.scalar, nc.gpsimd, nc.tensor
        N_CONST = 11
        PAIRS = B // 2
        TURN, GATE, MISC, SCORE, HEAD = 0, 2, 3, 4, 6
        cols_ps = PS[:, MISC, 0:ST * GR].rearrange("p (t g) -> p t g", t=ST)
        logit_ps = PS[:, MISC, 256:256 + ST * E].rearrange("p (t e) -> p t e", t=ST)
        head_ps = PS[:, HEAD:HEAD + 2, :].rearrange("p b (s c) -> p (b s) c", s=2)
        YB, HB, XB = 0, 4, 6

        def small(k, n=ST):
            return sm[:, k, 0:n]

        FULL0, LAST, FULL1 = (0, 4, 512), (HI - 1, 1, TAIL), (4, 4, 512)
        CHUNKS = [FULL0, LAST, FULL1]
        STEPS = len(CHUNKS) * HT
        TURNS = [(LAST, 0)] + [(FULL1, t) for t in range(4)] + [(FULL0, t) for t in range(4)]
        xbuf = {FULL0: xa, LAST: xt, FULL1: xb}

        passed = sem("passed")

        def wait_apart(eng, signal, value):
            eng.wait_ge(signal, value)
            eng.sem_inc(passed, 1)

        block = stack.enter_context(nc.Block())

        @block.sync
        def _(sp):
            sp.wait_ge(pool_const, 1)
            sp.dma_start(wload[0:NH, :], w_fg).then_inc(const_in, 16)
            sp.dma_start(wload[32:32 + NH, :], w_ig).then_inc(const_in, 16)
            sp.dma_start(gate_bias[0:NH, :], b_fg.rearrange("(h o) -> h o", o=1)).then_inc(const_in, 16)
            sp.dma_start(gate_bias[32:32 + NH, :], b_ig.rearrange("(h o) -> h o", o=1)).then_inc(const_in, 16)
            sp.dma_start(rload[:, :], w_router).then_inc(const_in, 16)
            sp.dma_start(bload[:, :], b1.rearrange("e (j p) -> (e j) p", p=P)).then_inc(const_in, 16)
            sp.dma_start(tanh_x[:, :], g_xattn.partition_broadcast(P)).then_inc(const_in, 16)
            sp.dma_start(tanh_f[:, :], g_ffn.partition_broadcast(P)).then_inc(const_in, 16)
            sp.dma_start(gvec[:, :], ln_w.partition_broadcast(P)).then_inc(const_in, 16)
            sp.dma_start(xn_dram[TOK:TOK + PAD, :], zeros[:, :]).then_inc(const_in, 16)
            sp.dma_start(out[TOK:TOK + PAD, :], zeros[:, :]).then_inc(const_in, 16)
            with sp.Fori(0, PAIRS) as i:
                wait_apart(sp, x1_stored, i * 32)
                wait_apart(sp, head_summed, i * 8)
                for p in range(2):
                    sp.dma_start(xs[p][:, :, :], x_rows[i * 2 + p]).then_inc(batch_in[p], 16)
                    for t in range(ST):
                        sp.dma_start(vs[p][:, t, :, 0:DH], ctx_rows[i * 2 + p, t]).then_inc(batch_in[p], 16)
                for p in range(2):
                    wait_apart(sp, negrow_made, i * 2 + (p + 1))
                    sp.dma_start(negmax_dram[i * 2 + p].rearrange("(h s) -> h s", h=NH), g_neg[:, :]).then_inc(negrow_out, 16)
                    wait_apart(sp, negrow_out, i * 32 + 16 * (p + 1))
                    wait_apart(sp, decay_made, i * 8)
                    sp.dma_start(negmax[p][:, :, :].rearrange("q h s -> q (h s)"),
                                 negmax_dram[i * 2 + p].partition_broadcast(P)).then_inc(negmax_in[p], 16)
                for p in range(2):
                    wait_apart(sp, x1_made, i * 2 + (p + 1))
                    sp.dma_start(out_rows[i * 2 + p], xs[p][:, :, :]).then_inc(x1_stored, 16)
                    wait_apart(sp, xn_made, i * 2 + (p + 1))
                    sp.dma_start(xn_rows[i * 2 + p], xn[:, :, :]).then_inc(xn_stored, 16)

            def load_weights(e, g, wait):
                if wait is not None:
                    wait_apart(sp, raw_used, wait)
                for jj in range(2):
                    j = 2 * g + jj
                    sp.dma_start(raw[:, g % 2, jj, 0:D].rearrange("p (k c) -> p k c", k=KT),
                                 w1[e].rearrange("(k p) n -> p k n", p=P)[:, :, j * P:(j + 1) * P]).then_inc(raw_in[g % 2], 16)
                sp.dma_start(raw[:, g % 2, :, D:2 * D],
                             w2[e, 2 * g * P:(2 * g + 2) * P, :].rearrange("(j p) n -> p j n", p=P)).then_inc(raw_in[g % 2], 16)

            for g in range(HT // 2):
                load_weights(0, g, None if g < 2 else 2 * (g - 1))

            def load_b2(e):
                wait_apart(sp, y_taken, e * HI)
                sp.dma_start(b2_row[:, :], b2[e].partition_broadcast(P)).then_inc(b2_in, 16)

            with sp.Fori(0, E - 1) as e:
                load_b2(e)
                for g in range(HT // 2):
                    load_weights(e + 1, g, e * HT + (HT + 2 * (g - 1)))
            load_b2(E - 1)
            sp.wait_ge(y_added, 16 * HI * E)
            sp.wait_ge(x1_stored, 16 * B)
            sp.wait_ge(xn_stored, 16 * B)
            sp.wait_ge(const_in, 16 * N_CONST)

        @block.gpsimd
        def _(pool):
            G.memset(wload[:, :], 0.0)
            G.memset(zeros[:, :], 0.0).then_inc(pool_const, 1)
            G.memset(ones[:, :], 1.0).then_inc(pool_const, 1)
            pool.wait_ge(pool_const, 2)
            G.affine_select(out=ident[:, :], in_=ones[:, 0:P], compare_op=ALU.is_equal, fill=0.0, base=0,
                            pattern=[[-1, P]], channel_multiplier=1).then_inc(pool_const, 1)
            for p in range(2):
                G.memset(vs[p][:, :, :, DH:VW], 1.0)
            G.affine_select(out=upper[:, :], in_=ones[:, 0:P], compare_op=ALU.is_gt, fill=0.0, base=0,
                            pattern=[[1, P]], channel_multiplier=-1)
            G.memset(g_rows[:, :], 0.0)
            G.iota(iota_e[:, :, :], pattern=[[0, NQ], [-1, E]], base=E, channel_multiplier=0,
                   allow_small_or_imprecise_dtypes=True)
            G.iota(iota_p[:, :], pattern=[[1, P]], base=0, channel_multiplier=0,
                   allow_small_or_imprecise_dtypes=True)
            G.iota(token[:, :].rearrange("p (k t) -> p k t", k=TOPK), pattern=[[0, TOPK], [P, TT]], base=-TOK,
                   channel_multiplier=1, allow_small_or_imprecise_dtypes=True)
            G.iota(pad_row[:, :], pattern=[[0, 1]], base=TOK, channel_multiplier=1,
                   allow_small_or_imprecise_dtypes=True).then_inc(pool_const, 1)
            with pool.Fori(0, PAIRS) as i:
                for n in range(2 * NH):
                    wait_apart(pool, decay_made, i * 8 + (n + 1))
                    diag = decay[n % 2][:, :, :].rearrange("p t s -> p (t s)")
                    diag = bass.AP(diag.tensor, diag.offset, [list(diag.ap[0]), [S + P, ST], [1, P]])
                    G.affine_select(out=diag, in_=diag, compare_op=ALU.is_ge, fill=0.0, base=0,
                                    pattern=[[0, ST], [1, P]], channel_multiplier=-1).then_inc(decay_masked, 1)

            pool.wait_ge(table_made, 2)
            pool.wait_ge(xn_stored, 16 * B)
            pool.wait_ge(x1_stored, 16 * B)
            pool.wait_ge(const_in, 16 * N_CONST)

            def gather(rows, n, ring, free):
                if free is not None:
                    wait_apart(pool, rows_turned, free)
                G.indirect_dma_start(out=gathered[0:n, ring, :], out_offset=None, in_=xn_dram[:, :],
                                     in_offset=bass.IndirectOffsetOnAxis(ap=rows[0:n, :], axis=0)
                                     ).then_inc(row_in[ring], 16)

            def add_rows(e, tile, n, u):
                wait_apart(pool, y_ready, e * HI + (u + 1))
                wait_apart(pool, y_added, e * (16 * HI) + 16 * u)
                G.indirect_dma_start(out=out[:, :], out_offset=bass.IndirectOffsetOnAxis(ap=rows_now[0:n, tile:tile + 1], axis=0),
                                     in_=y_out[0:n, u % 3, :], in_offset=None, compute_op=ALU.add,
                                     bounds_check=TOK + PAD - 1, oob_is_err=True).then_inc(y_added, 16)

            for t in range(4):
                gather(slot_row[:, t:t + 1], P, t % 3, None if t < 3 else t - 2)

            def expert(e, last):
                wait_apart(pool, y_added, e * (16 * HI))
                G.tensor_copy(rows_now[:, :], slot_row[:, bass.ds(e * HI, HI)]).then_inc(rows_copied, 1)
                wait_apart(pool, rows_copied, e + 1)
                for m in range(5):
                    chunk, t = TURNS[m]
                    n = TAIL if chunk is LAST else P
                    gather(rows_now[:, chunk[0] + t:chunk[0] + t + 1], n, (4 + m) % 3, e * HI + (m + 2))
                for u in range(4):
                    add_rows(e, u, P, u)
                add_rows(e, HI - 1, TAIL, 4)
                if not last:
                    G.tensor_copy(rows_next[:, :], slot_row[:, bass.ds(e * HI + HI, 4)]).then_inc(next_copied, 1)
                    wait_apart(pool, next_copied, e + 1)
                    for m in range(5, 9):
                        gather(rows_next[:, m - 5:m - 4], P, (4 + m) % 3, e * HI + (m + 2))
                for u in range(4):
                    add_rows(e, 4 + u, P, 5 + u)

            with pool.Fori(0, E - 1) as e:
                expert(e, False)
            expert(E - 1, True)

        @block.tensor
        def _(pe):
            pe.wait_ge(const_in, 16 * N_CONST)
            pe.wait_ge(pool_const, 4)
            for k in range(3 * KT):
                T.transpose(PS[:, 0, k * GR:(k + 1) * GR], wload[:, k * P:(k + 1) * P], ident[0:GR, 0:GR])
            for k in range(KT):
                T.transpose(PS[:, 1, k * E:(k + 1) * E], rload[:, k * P:(k + 1) * P], ident[0:E, 0:E])
            T.transpose(PS[:, 2, 0:P], bload[:, :], ident[:, :]).then_inc(weights_turned, 1)
            pe.wait_ge(consts_ready, 1)
            with pe.Fori(0, PAIRS) as i:
                def turn(pos, wide):
                    pe.wait_ge(turn_copied, i * 24 + max(pos - 1, 0))
                    for k in range(KT):
                        ins = T.transpose(PS[:, TURN + pos % 2, k * P:(k + 1) * P], wide[k], ident[:, :])
                    ins.then_inc(turn_made, 1)

                for p in range(2):
                    for t in range(ST):
                        pe.wait_ge(q_made, i * 8 + (4 * p + t + 1))
                        turn(8 * p + t, [qn[:, t, k * P:(k + 1) * P] for k in range(KT)])
                    pe.wait_ge(batch_in[p], i * 80 + 80)
                    for t in range(ST):
                        turn(8 * p + 4 + t, [vs[p][:, t, k, 0:DH] for k in range(KT)])
                    pe.wait_ge(turn_copied, i * 24 + 8 * (p + 1))
                    pe.wait_ge(gates_taken, i * 2 + p)
                    for k in range(2 * KT):
                        src = qT[p][:, k, :] if k < KT else kT[p][:, k - KT, :]
                        ins = T.matmul(PS[0:GR, GATE, :], wgate[:, k, :], src, start=(k == 0), stop=(k == 2 * KT - 1))
                    ins.then_inc(gates_made, 1)
                for p in range(2):
                    wait_apart(pe, gate_rows_made, i * 2 + (p + 1))
                    wait_apart(pe, cols_copied, i * 2 + p)
                    for t in range(ST):
                        ins = T.transpose(cols_ps[:, t, :], g_rows[:, t * P:(t + 1) * P], ident[0:GR, 0:GR])
                    ins.then_inc(cols_made, 1)

                def scores(n):
                    p, h = n // NH, n % NH
                    for t in range(ST):
                        pe.wait_ge(scored, i * 32 + max(4 * n + t - 1, 0))
                        T.matmul(PS[:, SCORE + t % 2, 0:S - t * P], kT[p][:, h, t * P:(t + 1) * P],
                                 qT[p][:, h, t * P:S], start=True, stop=True).then_inc(scores_made, 1)

                def outputs(n):
                    p, h = n // NH, n % NH
                    pe.wait_ge(head_copied, i * 8 + n)
                    for s in range(ST):
                        pe.wait_ge(scored, i * 32 + (4 * n + s + 1))
                        for t in range(s + 1):
                            ins = T.matmul(head_ps[:, s, 0:DH + 1], decay[n % 2][:, t, s * P:(s + 1) * P],
                                           vs[p][:, t, h, 0:DH + 1], start=(t == 0), stop=(t == s))
                    ins.then_inc(head_summed, 1)

                scores(0)
                for n in range(2 * NH):
                    if n + 1 < 2 * NH and n + 1 != NH:
                        scores(n + 1)
                    outputs(n)
                    if n + 1 == NH:
                        scores(n + 1)
                for p in range(2):
                    pe.wait_ge(xn_made, i * 2 + (p + 1))
                    for t in range(ST):
                        turn(16 + 4 * p + t, [xn[:, t, k * P:(k + 1) * P] for k in range(KT)])
                    pe.wait_ge(turn_copied, i * 24 + (20 + 4 * p))
                    pe.wait_ge(logits_copied, i * 2 + p)
                    for t in range(ST):
                        for k in range(KT):
                            ins = T.matmul(logit_ps[:, t, :], kT[p][:, k, t * P:(t + 1) * P], wrouter[:, k, :],
                                           start=(k == 0), stop=(k == KT - 1))
                    ins.then_inc(logits_made, 1)

            pe.wait_ge(choice_made, 1)
            flat = chosen[:, :, :].rearrange("p q e -> p (q e)")
            T.matmul(PS[:, 0, :], upper[:, :], flat, start=True, stop=True)
            T.matmul(PS[:, 1, :], ones[:, 0:P], flat, start=True, stop=True).then_inc(ranks_made, 1)
            for q in range(NQ):
                pe.wait_ge(onehot_made, q + 1)
                T.matmul(PS[:, 2, 0:2 * E * HI], one_lo[:, q % 4, :], hi_vals[:, q % 4, :, :].rearrange("p a h -> p (a h)"),
                         start=(q == 0), stop=(q == NQ - 1)).then_inc(onehot_used, 1)

            def turn_rows(chunk, t, bank, ring, landed, copied):
                n = TAIL if chunk is LAST else P
                wait_apart(pe, row_in[ring], landed)
                if copied is not None:
                    wait_apart(pe, x_ready, copied)
                for k in range(KT):
                    ins = T.transpose(PS[:, XB + bank, k * P:k * P + n], gathered[0:n, ring, k * P:(k + 1) * P], ident[0:n, 0:n])
                ins.then_inc(rows_turned, 1)

            def wait_step(eng, e, n):
                c, j = divmod(n, HT)
                if j == HT - 1:
                    eng.wait_ge(y_tile, e * HI + (4, 5, 9)[c])
                else:
                    eng.wait_ge(y_step, e * (3 * (HT - 1)) + (c * (HT - 1) + j + 1))

            pe.wait_ge(table_made, 2)
            for t in range(4):
                turn_rows(FULL0, t, t % 2, t % 3, 16 * (t // 3 + 1), None if t < 2 else t - 1)

            def expert(e, last):
                def first_layer(n):
                    chunk, j = CHUNKS[n // HT], n % HT
                    width = chunk[2] + chunk[2] % 2
                    if j == 0:
                        pe.wait_ge(x_ready, e * HI + (4, 5, 9)[n // HT])
                    pe.wait_ge(w_ready, e * (2 * HT) + (2 * j + 2))
                    if n >= 2:
                        pe.wait_ge(h_made, e * STEPS + (n - 1))
                    xh, xl = xbuf[chunk]
                    for k in range(KT):
                        for a, (w, v) in enumerate(((w_hi, xh), (w_hi, xl), (w_lo, xh))):
                            ins = T.matmul(PS[:, HB + n % 2, 0:width], w[:, j, k * P:(k + 1) * P], v[:, k, 0:width],
                                           start=(k == 0 and a == 0), stop=(k == KT - 1 and a == 2))
                    ins.then_inc(h_summed, 1)

                def second_layer(n):
                    chunk, j = CHUNKS[n // HT], n % HT
                    pe.wait_ge(h_split, e * (2 * STEPS) + (2 * n + 2))
                    for t in range(chunk[1]):
                        m = min(P, chunk[2] - t * P)
                        if j == 0:
                            pe.wait_ge(y_taken, e * HI + {0: 0, 1: 1, 2: 5}[n // HT])
                        for a, (h, w) in enumerate(((h_hi, w_hi), (h_hi, w_lo), (h_lo, w_hi))):
                            ins = T.matmul(PS[0:m, YB + t, :], h[:, n % 2, t * P:t * P + m], w[:, j, D:2 * D],
                                           start=(j == 0 and a == 0), stop=(j == HT - 1 and a == 2))
                        if j == HT - 1:
                            ins.then_inc(y_tile, 1)
                    if j < HT - 1:
                        ins.then_inc(y_step, 1)

                turn_at = {5: 0, 7: 1, 9: 2, 11: 3, 13: 4}
                if not last:
                    turn_at.update({2 * HT + 2: 5, 2 * HT + 4: 6, 2 * HT + 6: 7, 2 * HT + 8: 8})
                first_layer(0)
                for n in range(STEPS):
                    if n + 1 < STEPS:
                        first_layer(n + 1)
                    if n in turn_at:
                        m = turn_at[n]
                        chunk, t = TURNS[m]
                        turn_rows(chunk, t, m % 2, (4 + m) % 3, e * (16 * 3) + 16 * ((4 + m) // 3 + 1), e * HI + (4 + max(m - 1, 0)))
                    second_layer(n)

            with pe.Fori(0, E - 1) as e:
                expert(e, False)
            expert(E - 1, True)

        @block.scalar
        def _(act):
            act.wait_ge(const_in, 16 * N_CONST)
            A.activation(tanh_x[:, :], tanh_x[:, :], ACT.Tanh)
            A.activation(tanh_f[:, :], tanh_f[:, :], ACT.Tanh).then_inc(tanh_made, 1)
            with act.Fori(0, PAIRS) as i:
                chain = Chain(act, a_chain, i, 8)

                def seed(pos):
                    act.wait_ge(ln_var_made, i * 6 + (pos + 1))
                    chain(A.activation(small(3, ST * NH), small(2, ST * NH), ACT.Ln))
                    A.activation(small(3, ST * NH), small(3, ST * NH), ACT.Exp, scale=-0.5).then_inc(ln_seed_made, 1)

                def copy_turn(pos, dst):
                    act.wait_ge(turn_made, i * 24 + (pos + 1))
                    A.copy(dst, PS[:, TURN + pos % 2, :].rearrange("p (k c) -> p k c", k=KT)).then_inc(turn_copied, 1)

                def exponentials(n):
                    p, h = n // NH, n % NH
                    if h == 0:
                        act.wait_ge(cols_copied, i * 2 + (p + 1))
                        act.wait_ge(negmax_in[p], i * 16 + 16)
                    act.wait_ge(head_summed, i * 8 + max(n - 1, 0))
                    for t in range(ST):
                        ins = A.activation(decay[n % 2][:, t, t * P:S], negmax[p][:, h, t * P:S], ACT.Exp,
                                           bias=cols[p][:, t, h:h + 1])
                    ins.then_inc(decay_made, 1)

                def copy_head(n):
                    act.wait_ge(head_summed, i * 8 + (n + 1))
                    if n % NH == 0:
                        act.wait_ge(x1_made, i * 2 + n // NH)
                    A.copy(heads[:, :, n % NH, 0:DH + 1], head_ps[:, :, 0:DH + 1]).then_inc(head_copied, 1)

                seed(0)
                seed(1)
                for p in range(2):
                    for t in range(2 * ST):
                        dst = qT[p] if t < ST else kT[p]
                        copy_turn(8 * p + t, dst[:, :, (t % ST) * P:(t % ST + 1) * P])
                for p in range(2):
                    act.wait_ge(abs_made, i * 2 + (p + 1))
                    chain(A.activation(g_t[:, :], g_t[:, :], ACT.Exp, scale=-1.0))
                    A.activation(g_t[:, :], g_t[:, :], ACT.Ln, bias=1.0).then_inc(softplus_made, 1)
                    act.wait_ge(cols_copied, i * 2 + (p + 1))
                    A.activation(expneg[p][:, :, :], cols[p][:, :, 32:32 + NH], ACT.Exp).then_inc(expneg_made, 1)
                for n in range(2 * NH):
                    exponentials(n)
                    if n > 0:
                        copy_head(n - 1)
                    if n == NH:
                        seed(2)
                        seed(3)
                copy_head(2 * NH - 1)
                for t in range(ST):
                    copy_turn(16 + t, kT[0][:, :, t * P:(t + 1) * P])
                seed(4)
                seed(5)
                for t in range(ST):
                    copy_turn(20 + t, kT[1][:, :, t * P:(t + 1) * P])
                assert chain.n == 8, chain.n
            act.wait_ge(b_sub, 1)
            A.activation(prob[:, :, :], prob[:, :, :], ACT.Exp).then_inc(b_exp, 1)

            def upper_x(chunk, t, bank, turned):
                n = TAIL if chunk is LAST else P
                act.wait_ge(rows_turned, turned)
                A.copy(xbuf[chunk][0][:, :, t * P:t * P + n],
                       PS[:, XB + bank, :].rearrange("p (k c) -> p k c", k=KT)[:, :, 0:n]).then_inc(x_upper, 1)

            act.wait_ge(table_made, 2)
            for t in range(4):
                upper_x(FULL0, t, t % 2, t + 1)

            def expert(e, last):
                act.wait_ge(h_made, e * STEPS)
                A.copy(b1_now[:, :], b1_all[:, bass.ds(e * HT, HT)]).then_inc(b1_copied, 1)
                act.wait_ge(b1_copied, e + 1)
                turn_at = {5: 0, 7: 1, 9: 2, 11: 3, 13: 4}
                if not last:
                    turn_at.update({2 * HT + 2: 5, 2 * HT + 4: 6, 2 * HT + 6: 7, 2 * HT + 8: 8})
                for n in range(STEPS):
                    chunk = CHUNKS[n // HT]
                    act.wait_ge(h_summed, e * STEPS + (n + 1))
                    if n >= 2:
                        act.wait_ge(h_split, e * (2 * STEPS) + 2 * (n - 1))
                    A.activation(h_raw[:, n % 2, 0:chunk[2]], PS[:, HB + n % 2, 0:chunk[2]], ACT.Gelu,
                                 bias=b1_now[:, n % HT:n % HT + 1]).then_inc(h_made, 1)
                    if n in turn_at:
                        m = turn_at[n]
                        upper_x(*TURNS[m], m % 2, e * HI + (4 + m + 1))

            with act.Fori(0, E - 1) as e:
                expert(e, False)
            expert(E - 1, True)

        @block.vector
        def _(dve):
            link = Chain(dve, v_setup)
            dve.wait_ge(weights_turned, 1)
            wt = PS[:, 0, 0:3 * KT * GR].rearrange("p (k g) -> p k g", g=GR)
            link(V.tensor_copy(wgate[:, :, :], wt[:, 0:2 * KT, :]))
            link(V.tensor_tensor(wgate[:, KT:2 * KT, :], wgate[:, KT:2 * KT, :], wt[:, 2 * KT:3 * KT, :], ALU.add))
            link(V.tensor_copy(wrouter[:, :, :], PS[:, 1, 0:KT * E].rearrange("p (k e) -> p k e", e=E)))
            link(V.tensor_copy(b1_all[:, :], PS[:, 2, 0:P]))
            dve.wait_ge(tanh_made, 1)
            link(V.tensor_scalar(gvec[:, :], gvec[:, :], 1.0, tanh_x[:, 0:1], ALU.add, ALU.mult))
            V.memset(sm[:, :, :], 1.0).then_inc(consts_ready, 1)
            dve.wait_ge(consts_ready, 1)

            V_TURN = 66
            with dve.Fori(0, PAIRS) as i:
                chain = Chain(dve, v_chain, i, V_TURN)

                def inverse_root(pos, n):
                    dve.wait_ge(ln_seed_made, i * 6 + (pos + 1))
                    chain(V.tensor_tensor(small(4, n), small(3, n), small(2, n), ALU.mult))
                    chain(V.tensor_tensor(small(4, n), small(4, n), small(3, n), ALU.mult))
                    chain(V.tensor_scalar(small(4, n), small(4, n), -0.5, 1.5, ALU.mult, ALU.add))
                    chain(V.tensor_tensor(small(3, n), small(3, n), small(4, n), ALU.mult))

                mv = sm[:, 0:2, 0:ST].rearrange("p a t -> p t a")

                def layer_norm(src, dst, pos, signal, ready):
                    for t in range(ST):
                        ins = V.bn_stats(st6[:, t, :], src[:, t, :])
                    chain(ins)
                    dve.sem_inc(passed, 1)
                    for t in range(ST):
                        ins = V.bn_aggr(mv[:, t, :], st6[:, t, :])
                    chain(ins)
                    V.tensor_scalar(small(2), small(1), LN_EPS, None, ALU.add).then_inc(ln_var_made, 1)
                    inverse_root(pos, ST)
                    ready()
                    for t in range(ST):
                        ins = V.tensor_scalar(dst[:, t, :], src[:, t, :], sm[:, 0, t:t + 1], sm[:, 3, t:t + 1], ALU.subtract, ALU.mult)
                        if signal is q_made:
                            ins.then_inc(q_made, 1)
                    if signal is not q_made:
                        ins.then_inc(signal, 1)

                for p in range(2):
                    dve.wait_ge(batch_in[p], i * 80 + 80)
                    layer_norm(xs[p], qn, p, q_made, lambda: dve.wait_ge(turn_made, i * 24 + 4 * p))
                    dve.wait_ge(q_made, i * 8 + 4 * (p + 1))

                for p in range(2):
                    dve.wait_ge(gates_made, i * 2 + (p + 1))
                    gates = PS[:, GATE, :]
                    V.tensor_scalar(g_f[:, :], gates[0:NH, :], gate_bias[0:NH, 0:1], None, ALU.add)
                    chain(V.tensor_scalar(g_i[:, :], gates[32:32 + NH, :], gate_bias[32:32 + NH, 0:1], None, ALU.add))
                    V.scalar_tensor_tensor(g_t[:, :], g_f[:, :], -1.0, g_f[:, :], ALU.mult, ALU.max).then_inc(abs_made, 1)
                    dve.sem_inc(gates_taken, 1)
                    dve.wait_ge(softplus_made, i * 2 + (p + 1))
                    chain(V.scalar_tensor_tensor(g_f[:, :], g_f[:, :], 0.0, g_t[:, :], ALU.min, ALU.subtract))
                    chain(V.tensor_tensor_scan(g_cum[:, :], ones[0:NH, :], g_f[:, :], 0.0, ALU.mult, ALU.add))
                    chain(V.tensor_tensor(g_i[:, :], g_i[:, :], g_cum[:, :], ALU.subtract))
                    chain(V.tensor_tensor_scan(g_max[:, :], ones[0:NH, :], g_i[:, :], LOWEST, ALU.mult, ALU.max))
                    dve.wait_ge(negrow_out, i * 32 + 16 * p)
                    dve.wait_ge(cols_made, i * 2 + p)
                    V.tensor_scalar(g_neg[:, :], g_max[:, :], -1.0, None, ALU.mult).then_inc(negrow_made, 1)
                    V.tensor_copy(g_rows[0:NH, :], g_i[:, :])
                    V.scalar_tensor_tensor(g_rows[32:32 + NH, :], g_cum[:, :], -1.0, g_max[:, :], ALU.mult, ALU.subtract)\
                        .then_inc(gate_rows_made, 1)
                    dve.wait_ge(cols_made, i * 2 + (p + 1))
                    V.tensor_copy(cols[p][:, :, :], cols_ps).then_inc(cols_copied, 1)

                def weigh(n):
                    dve.wait_ge(decay_masked, i * 8 + (n + 1))
                    for t in range(ST):
                        dve.wait_ge(scores_made, i * 32 + (4 * n + t + 1))
                        d = decay[n % 2][:, t, t * P:S]
                        V.scalar_tensor_tensor(d, PS[:, SCORE + t % 2, 0:S - t * P], SCORE_SCALE, d, ALU.mult, ALU.mult)\
                            .then_inc(scored, 1)

                def finish(p):
                    n = ST * NH
                    dve.wait_ge(head_copied, i * 8 + 4 * (p + 1))
                    for t in range(ST):
                        for h in range(NH):
                            ins = V.bn_stats(st6[:, t * NH + h, :], heads[:, t, h, 0:DH])
                    chain(ins)
                    dve.wait_ge(expneg_made, i * 2 + (p + 1))
                    sums = heads[:, :, :, DH]
                    r = small(5, n).rearrange("p (t h) -> p t h", t=ST)
                    chain(V.scalar_tensor_tensor(r, sums, -1.0, sums, ALU.mult, ALU.max))
                    chain(V.tensor_tensor(r, r, expneg[p][:, :, :], ALU.max))
                    chain(V.tensor_scalar(small(5, n), small(5, n), NORM_EPS, None, ALU.add))
                    V.reciprocal(small(5, n), small(5, n))
                    V.tensor_tensor(small(6, n), st6[:, :, 1], st6[:, :, 4], ALU.add)
                    V.tensor_tensor(small(7, n), st6[:, :, 1], st6[:, :, 4], ALU.subtract)
                    chain(V.tensor_tensor(small(8, n), st6[:, :, 2], st6[:, :, 5], ALU.add))
                    V.tensor_scalar(small(6, n), small(6, n), 0.5, None, ALU.mult)
                    chain(V.scalar_tensor_tensor(small(7, n), small(7, n), 0.25, small(7, n), ALU.mult, ALU.mult))
                    chain(V.scalar_tensor_tensor(small(7, n), small(8, n), 1.0 / DH, small(7, n), ALU.mult, ALU.add))
                    chain(V.tensor_tensor(small(7, n), small(7, n), small(5, n), ALU.mult))
                    chain(V.tensor_tensor(small(7, n), small(7, n), small(5, n), ALU.mult))
                    V.tensor_scalar(small(2, n), small(7, n), LN_EPS, None, ALU.add).then_inc(ln_var_made, 1)
                    inverse_root(2 + 2 * p, n)
                    chain(V.tensor_tensor(small(9, n), small(3, n), small(5, n), ALU.mult))
                    for t in range(ST):
                        for h in range(NH):
                            k = t * NH + h
                            ins = V.tensor_scalar(heads[:, t, h, 0:DH], heads[:, t, h, 0:DH], sm[:, 6, k:k + 1], sm[:, 9, k:k + 1],
                                                  ALU.subtract, ALU.mult)
                    chain(ins)
                    dve.wait_ge(turn_made, i * 24 + 20 * p)
                    dve.wait_ge(xn_stored, i * 32 + 16 * p)
                    for t in range(ST):
                        ins = V.tensor_tensor(xn[:, t, :].rearrange("p (h c) -> p h c", h=NH), heads[:, t, :, 0:DH],
                                              gvec[:, :].rearrange("p (h c) -> p h c", h=NH), ALU.mult)
                    chain(ins)
                    for t in range(ST):
                        ins = V.tensor_tensor(xs[p][:, t, :], xs[p][:, t, :], xn[:, t, :], ALU.add)
                    ins.then_inc(x1_made, 1)
                    dve.wait_ge(x1_made, i * 2 + (p + 1))
                    layer_norm(xs[p], xn, 3 + 2 * p, xn_made, lambda: None)

                for n in range(NH):
                    weigh(n)
                finish(0)
                for n in range(NH, 2 * NH):
                    weigh(n)
                finish(1)
                for p in range(2):
                    dve.wait_ge(logits_made, i * 2 + (p + 1))
                    V.tensor_copy(logits[:, bass.ds(i * 8 + 4 * p, ST), :], logit_ps).then_inc(logits_copied, 1)
                assert chain.n == V_TURN, ("V_TURN", chain.n)

            link = Chain(dve, b_chain)
            top = rb[:, 0, :]
            dve.wait_ge(logits_copied, B)

            def over_e(v, n):
                return v.rearrange("p (q o) -> p q o", o=1).to_broadcast([P, n, E])

            link(V.tensor_reduce(rb[:, 1, 0:TT], logits[:, :, :], AX.X, ALU.max))
            V.tensor_tensor(prob[:, :, :], logits[:, :, :], over_e(rb[:, 1, 0:TT], TT), ALU.subtract).then_inc(b_sub, 1)
            dve.wait_ge(b_exp, 1)
            link(V.tensor_reduce(rb[:, 1, 0:TT], prob[:, :, :], AX.X, ALU.add))
            link(V.reciprocal(rb[:, 1, 0:TT], rb[:, 1, 0:TT]))
            link(V.tensor_tensor(prob[:, :, :], prob[:, :, :], over_e(rb[:, 1, 0:TT], TT), ALU.mult))
            for k in range(TOPK):
                q0, q1 = k * TT, (k + 1) * TT
                first = iota_e[:, q0:q1, :]
                link(V.tensor_reduce(top[:, q0:q1], prob[:, :, :], AX.X, ALU.max))
                link(V.tensor_tensor(work[:, q0:q1, :], prob[:, :, :], over_e(top[:, q0:q1], TT), ALU.is_equal))
                link(V.tensor_tensor(work[:, q0:q1, :], work[:, q0:q1, :], first, ALU.mult))
                link(V.tensor_reduce(rb[:, 2, q0:q1], work[:, q0:q1, :], AX.X, ALU.max))
                link(V.tensor_tensor(chosen[:, q0:q1, :], first, over_e(rb[:, 2, q0:q1], TT), ALU.is_equal))
                if k == 0:
                    link(V.scalar_tensor_tensor(prob[:, :, :], chosen[:, q0:q1, :], -2.0, prob[:, :, :], ALU.mult, ALU.add))
            dve.sem_inc(choice_made, 1)
            dve.wait_ge(ranks_made, 1)
            link(V.tensor_copy(work[:, :, :], PS[:, 1, :].rearrange("p (q e) -> p q e", e=E)))
            for ex in range(E):
                ins = V.tensor_tensor_scan(base[:, :, ex], ones[:, 0:NQ], work[:, :, ex], 0.0, ALU.mult, ALU.add)
            link(ins)
            link(V.tensor_tensor(base[:, :, :], base[:, :, :], work[:, :, :], ALU.subtract))
            link(V.tensor_tensor(base[:, :, :], base[:, :, :], PS[:, 0, :].rearrange("p (q e) -> p q e", e=E), ALU.add))
            link(V.tensor_tensor(base[:, :, :], base[:, :, :], chosen[:, :, :], ALU.mult))
            link(V.tensor_reduce(rb[:, 3, :], base[:, :, :], AX.X, ALU.add))
            link(V.tensor_copy(rb_i[:, 0, :], rb[:, 3, :]))
            V.tensor_scalar(rb_i[:, 1, :], rb_i[:, 0, :], 7, None, ALU.arith_shift_right)
            link(V.tensor_scalar(rb_i[:, 2, :], rb_i[:, 0, :], P - 1, None, ALU.bitwise_and))
            V.tensor_copy(rb[:, 4, :], rb_i[:, 1, :])
            link(V.tensor_copy(rb[:, 5, :], rb_i[:, 2, :]))
            link(V.tensor_scalar(rb[:, 2, :], rb[:, 2, :], -float(HI), float(E * HI), ALU.mult, ALU.add))
            link(V.tensor_tensor(rb[:, 4, :], rb[:, 4, :], rb[:, 2, :], ALU.add))
            link(V.tensor_scalar(rb[:, 3, :], rb[:, 3, :], float(CAP), DROPPED, ALU.is_ge, ALU.mult))
            link(V.tensor_tensor(rb[:, 4, :], rb[:, 4, :], rb[:, 3, :], ALU.add))
            V.tensor_tensor(rb[:, 6, :], token[:, :], rb[:, 5, :], ALU.subtract)
            link(V.tensor_scalar(rb[:, 7, :], top, tanh_f[:, 0:1], None, ALU.mult))
            for q in range(NQ):
                if q >= 4:
                    dve.wait_ge(onehot_used, q - 3)
                V.tensor_scalar(one_lo[:, q % 4, :], iota_p[:, :], rb[:, 5, q:q + 1], None, ALU.is_equal)
                for a in range(2):
                    ins = V.tensor_scalar(hi_vals[:, q % 4, a, :], iota_p[:, 0:E * HI], rb[:, 4, q:q + 1], rb[:, 6 + a, q:q + 1],
                                          ALU.is_equal, ALU.mult)
                ins.then_inc(onehot_made, 1)
            dve.wait_ge(onehot_used, NQ)
            link(V.tensor_scalar(row_f[:, :], PS[:, 2, 0:E * HI], pad_row[:, 0:1], None, ALU.add))
            V.tensor_copy(slot_row[:, :], row_f[:, :]).then_inc(table_made, 1)
            V.tensor_copy(slot_weight[:, :], PS[:, 2, E * HI:2 * E * HI]).then_inc(table_made, 1)
            dve.wait_ge(table_made, 2)

            def split_weights(e, j, raw_arrived, last_use):
                g, jj = j // 2, j % 2
                if jj == 0:
                    dve.wait_ge(raw_in[g % 2], raw_arrived)
                if last_use is not None:
                    last_use()
                V.tensor_copy(w_hi[:, j, :], raw[:, g % 2, jj, :]).then_inc(w_ready, 1)
                dve.wait_ge(w_ready, e * (2 * HT) + (2 * j + 1))
                V.tensor_tensor(w_lo[:, j, :], raw[:, g % 2, jj, :], w_hi[:, j, :].bitcast(F32), ALU.subtract).then_inc(w_ready, 1)
                dve.wait_ge(w_ready, e * (2 * HT) + (2 * j + 2))
                dve.sem_inc(raw_used, 1)

            def rest_of_x(chunk, t, bank, count):
                n = TAIL if chunk is LAST else P
                hi, lo = xbuf[chunk]
                dve.wait_ge(x_upper, count)
                V.tensor_tensor(lo[:, :, t * P:t * P + n], PS[:, XB + bank, :].rearrange("p (k c) -> p k c", k=KT)[:, :, 0:n],
                                hi[:, :, t * P:t * P + n].bitcast(F32), ALU.subtract).then_inc(x_ready, 1)

            def wait_step(e, n):
                c, j = divmod(n, HT)
                if j == HT - 1:
                    dve.wait_ge(y_tile, e * HI + (4, 5, 9)[c])
                else:
                    dve.wait_ge(y_step, e * (3 * (HT - 1)) + (c * (HT - 1) + j + 1))

            dve.wait_ge(x1_stored, 16 * B)
            dve.wait_ge(xn_stored, 16 * B)
            for buf in xt:
                V.memset(buf[:, :, :].bitcast(F32), 0.0)
            for t in range(4):
                rest_of_x(FULL0, t, t % 2, t + 1)
            for j in range(HT):
                split_weights(0, j, 48 * (j // 4 + 1), None)

            def expert(e, last):
                dve.wait_ge(y_ready, e * HI)
                V.tensor_copy(weight_now[:, :], slot_weight[:, bass.ds(e * HI, HI)]).then_inc(weight_copied, 1)
                dve.wait_ge(weight_copied, e + 1)
                dve.wait_ge(rows_copied, e + 1)
                turn_at = {5: 0, 7: 1, 9: 2, 11: 3, 13: 4}
                if not last:
                    turn_at.update({2 * HT + 2: 5, 2 * HT + 4: 6, 2 * HT + 6: 7, 2 * HT + 8: 8})
                done = 0

                def split_hidden(n):
                    width = CHUNKS[n // HT][2]
                    dve.wait_ge(h_made, e * STEPS + (n + 1))
                    if n >= 2:
                        wait_step(e, n - 2)
                    V.tensor_copy(h_hi[:, n % 2, 0:width], h_raw[:, n % 2, 0:width]).then_inc(h_split, 1)
                    dve.wait_ge(h_split, e * (2 * STEPS) + (2 * n + 1))
                    V.tensor_tensor(h_lo[:, n % 2, 0:width], h_raw[:, n % 2, 0:width], h_hi[:, n % 2, 0:width].bitcast(F32),
                                    ALU.subtract).then_inc(h_split, 1)

                def take(c):
                    chunk = CHUNKS[c]
                    u0 = (0, 4, 5)[c]
                    for t in range(chunk[1]):
                        u, m = u0 + t, min(P, chunk[2] - t * P)
                        dve.wait_ge(y_tile, e * HI + (u + 1))
                        if u == 0:
                            dve.wait_ge(b2_in, e * 16 + 16)
                        if u >= 3:
                            dve.wait_ge(y_added, e * (16 * HI) + 16 * (u - 2))
                        V.tensor_tensor(y_out[0:m, u % 3, :], PS[0:m, YB + t, :], b2_row[0:m, :], ALU.add).then_inc(y_taken, 1)
                        dve.wait_ge(y_taken, e * HI + (u + 1))
                        V.tensor_scalar(y_out[0:m, u % 3, :], y_out[0:m, u % 3, :], weight_now[0:m, chunk[0] + t:chunk[0] + t + 1], None,
                                        ALU.mult).then_inc(y_ready, 1)

                for n in range(STEPS):
                    split_hidden(n)
                    if n in turn_at:
                        m = turn_at[n]
                        rest_of_x(*TURNS[m], m % 2, e * HI + (4 + m + 1))
                    if n % HT == 0 and n > 0:
                        take(n // HT - 1)
                    if not last and n >= 2 * HT + 2:
                        j = n - 2 * HT - 2
                        split_weights(e + 1, j, e * 192 + (192 + 48 * (j // 4 + 1)), lambda: wait_step(e, 2 * HT + j))
                take(2)
                if not last:
                    for j in (HT - 2, HT - 1):
                        split_weights(e + 1, j, e * 192 + (192 + 48 * (j // 4 + 1)), lambda: wait_step(e, 2 * HT + j))

            with dve.Fori(0, E - 1) as e:
                expert(e, False)
            expert(E - 1, True)


_INS = ['x', 'ctx_1024', 'g_xattn', 'g_ffn', 'L0_xattn_w_igate', 'L0_xattn_b_igate', 'L0_xattn_w_fgate',
        'L0_xattn_b_fgate', 'L0_xattn_ln_weight', 'L0_ffn_Wg', 'L0_ffn_W1', 'L0_ffn_b1', 'L0_ffn_W2', 'L0_ffn_b2']


def kernel(**inputs):
    import numpy as _np
    import concourse.bacc as _bacc
    from concourse import mybir as _mybir
    from concourse.bass_utils import run_bass_kernel_spmd as _run

    nc = _bacc.Bacc("TRN2", target_bir_lowering=False, num_devices=1)
    arrays, args = {}, []
    for name in _INS:
        a = _np.ascontiguousarray(inputs[name])
        arrays[f"in_{name}_dram"] = a
        args.append(nc.dram_tensor(f"in_{name}_dram", a.shape, _mybir.dt.from_np(a.dtype), kind="ExternalInput").ap())
    args.append(nc.dram_tensor("out_0_dram", (TOK + PAD, D), _mybir.dt.float32, kind="ExternalOutput").ap())
    build(nc, *args)
    r = _run(nc, [arrays], core_ids=[0])
    return r.results[0]["out_0_dram"][0:TOK].reshape(B, S, D)
```

```python
from contextlib import ExitStack

import concourse.bass as bass
from concourse import mybir

F32 = mybir.dt.float32
F32R = mybir.dt.float32r
I32 = mybir.dt.int32
U32 = mybir.dt.uint32
ALU = mybir.AluOpType
ACT = mybir.ActivationFunctionType
AX = mybir.AxisListType

P = 128
B, S, D = 8, 512, 512
NH = 4
DH = D // NH
ST = S // P
KT = D // P
E = 8
HID = 2048
HT = HID // P
TOK = B * S
TT = TOK // P
TOPK = 2
CAP = int(round(TOPK * TOK * 1.05 / E))
HI = -(-CAP // P)
RT = 2 * -(-CAP // (2 * HI))
CT = 3
NC = HI // CT
CW = CT * RT
assert HI == CT * NC and CW <= 512 and CAP <= HI * RT
PAD = P
NQ = TOPK * TT
LN_EPS = 1e-5
NORM_EPS = 1e-6
SCORE_SCALE = float(DH) ** -0.5
VW = DH + 2
GR = 36
DROPPED = 1000.0
LOWEST = -3.0e38
ROUND = 1.5 * 2 ** 23
START = 1


class Chain:

    def __init__(self, engine, signal, turn=0, per_turn=0):
        self.engine, self.sem, self.turn, self.per_turn, self.n = engine, signal, turn, per_turn, 0

    def __call__(self, ins):
        self.n += 1
        ins.then_inc(self.sem, 1)
        self.engine.wait_ge(self.sem, self.turn * self.per_turn + self.n)

    def closed(self):
        assert self.n == self.per_turn, (self.sem, self.n)


def build(nc, x, ctx_in, g_xattn, g_ffn, w_ig, b_ig, w_fg, b_fg, ln_w, w_router, w1, b1, w2, b2, out):
    x_rows = x.rearrange("b (t p) d -> b p t d", p=P)
    ctx_rows = ctx_in.rearrange("b (t p) (h c) -> b t p h c", p=P, h=NH)
    xn_dram = nc.dram_tensor("xn_rows", (TOK + PAD, D), F32, kind="Internal").ap()
    negmax_dram = nc.dram_tensor("negmax_rows", (B, NH * S), F32, kind="Internal").ap()
    out_rows = out[0:TOK, :].rearrange("(b t p) d -> b p t d", b=B, p=P)
    xn_rows = xn_dram[0:TOK, :].rearrange("(b t p) d -> b p t d", b=B, p=P)

    stack = ExitStack()
    with stack:
        def sb(name, shape, dt=F32, where=stack):
            return where.enter_context(nc.sbuf_tensor(name, shape, dt))

        def sem(name):
            return stack.enter_context(nc.semaphore(name))

        PS = stack.enter_context(nc.psum_tensor("PS", [P, 8, 512], F32))

        ident = sb("ident", [P, P])
        b1_all = sb("b1_all", [P, E * HT])
        slot_row = sb("slot_row", [P, E * HI], I32)
        slot_weight = sb("slot_weight", [P, E * HI])

        a_mem = ExitStack()
        ones = sb("ones", [P, S], F32, a_mem)
        zeros = sb("zeros", [P, D], F32, a_mem)
        logits = sb("logits", [P, TT, E], F32, a_mem)
        gate_bias = sb("gate_bias", [GR, 1], F32, a_mem)
        tanh_x = sb("tanh_x", [P, 1], F32, a_mem)
        wrouter = sb("wrouter", [P, KT, E], F32, a_mem)
        wgate = sb("wgate", [P, 2 * KT, GR], F32, a_mem)
        tanh_f = sb("tanh_f", [P, 1], F32, a_mem)
        xs = [sb(f"xs{p}", [P, ST, D], F32, a_mem) for p in range(2)]
        vs = [sb(f"vs{p}", [P, ST, NH, VW], F32, a_mem) for p in range(2)]
        qn = sb("qn", [P, ST, D], F32, a_mem)
        qT = [sb(f"qT{p}", [P, KT, S], F32, a_mem) for p in range(2)]
        kT = [sb(f"kT{p}", [P, KT, S], F32, a_mem) for p in range(2)]
        decay = [sb(f"decay{p}", [P, ST, S], F32, a_mem) for p in range(2)]
        negmax = [sb(f"negmax{p}", [P, NH, S], F32, a_mem) for p in range(2)]
        heads = sb("heads", [P, ST, NH, VW], F32, a_mem)
        xn = sb("xn", [P, ST, D], F32, a_mem)
        gvec = sb("gvec", [P, D], F32, a_mem)
        g_f = sb("g_f", [NH, S], F32, a_mem)
        g_i = sb("g_i", [NH, S], F32, a_mem)
        g_t = sb("g_t", [NH, S], F32, a_mem)
        g_cum = sb("g_cum", [NH, S], F32, a_mem)
        g_max = sb("g_max", [NH, S], F32, a_mem)
        g_rows = sb("g_rows", [GR, S], F32, a_mem)
        g_neg = sb("g_neg", [NH, S], F32, a_mem)
        cols = [sb(f"cols{p}", [P, ST, GR], F32, a_mem) for p in range(2)]
        expneg = [sb(f"expneg{p}", [P, ST, NH], F32, a_mem) for p in range(2)]
        st6 = sb("st6", [P, ST * NH, 6], F32, a_mem)
        sm = sb("sm", [P, 10, ST * NH], F32, a_mem)
        wload = sb("wload", [GR, 3 * D], F32, a_mem)
        rload = sb("rload", [E, D], F32, a_mem)
        bload = sb("bload", [E * HT, P], F32, a_mem)
        iota_e = sb("iota_e", [P, NQ, E], F32, a_mem)
        iota_p = sb("iota_p", [P, P], F32, a_mem)
        token = sb("token", [P, NQ], F32, a_mem)
        upper = sb("upper", [P, P], F32, a_mem)
        prob = sb("prob", [P, TT, E], F32, a_mem)
        work = sb("work", [P, NQ, E], F32, a_mem)
        chosen = sb("chosen", [P, NQ, E], F32, a_mem)
        base = sb("base", [P, NQ, E], F32, a_mem)
        rb = sb("rb", [P, 8, NQ], F32, a_mem)
        one_lo = sb("one_lo", [P, 4, P], F32, a_mem)
        hi_vals = sb("hi_vals", [P, 4, 2, E * HI], F32, a_mem)
        pad_row = sb("pad_row", [P, 1], F32, a_mem)
        row_f = sb("row_f", [P, E * HI], F32, a_mem)
        a_mem.close()

        w_hi = sb("w_hi", [P, HT, 2 * D], F32R)
        w_lo = sb("w_lo", [P, HT, 2 * D], F32R)
        x_hi = sb("x_hi", [P, NC, KT, CW], F32R)
        x_lo = sb("x_lo", [P, NC, KT, CW], F32R)
        h_raw = sb("h_raw", [P, 3, CW])
        h_hi = sb("h_hi", [P, 3, CW], F32R)
        h_lo = sb("h_lo", [P, 3, CW], F32R)
        y_out = sb("y_out", [P, CT, D])
        b2_row = sb("b2_row", [P, D])
        b1_now = sb("b1_now", [P, HT])
        weight_now = sb("weight_now", [P, HI])
        rows_add = [sb(f"rows_add{t}", [P, 1], I32) for t in range(CT)]
        rows_turn = sb("rows_turn", [P, HI], I32)
        raw = sb("raw", [P, 2, 4 * D])
        gathered = sb("gathered", [P, 3, D])

        const_in = sem("const_in")
        pool_const = sem("pool_const")
        weights_turned = sem("weights_turned")
        consts_ready = sem("consts_ready")
        tanh_made = sem("tanh_made")
        v_setup = sem("v_setup")
        batch_in = [sem(f"batch_in{p}") for p in range(2)]
        ln_var_made = sem("ln_var_made")
        ln_seed_made = sem("ln_seed_made")
        q_made = sem("q_made")
        turn_made = sem("turn_made")
        turn_copied = sem("turn_copied")
        gates_made = sem("gates_made")
        gates_taken = sem("gates_taken")
        abs_made = sem("abs_made")
        softplus_made = sem("softplus_made")
        negrow_made = sem("negrow_made")
        negrow_out = sem("negrow_out")
        negmax_in = [sem(f"negmax_in{p}") for p in range(2)]
        gate_rows_made = sem("gate_rows_made")
        cols_made = sem("cols_made")
        cols_copied = sem("cols_copied")
        expneg_made = sem("expneg_made")
        decay_made = sem("decay_made")
        decay_masked = sem("decay_masked")
        scores_made = sem("scores_made")
        scored = sem("scored")
        head_summed = sem("head_summed")
        head_copied = sem("head_copied")
        x1_made = sem("x1_made")
        xn_made = sem("xn_made")
        x1_stored = sem("x1_stored")
        xn_stored = sem("xn_stored")
        xn_free = sem("xn_free")
        logits_made = sem("logits_made")
        logits_copied = sem("logits_copied")
        v_chain = sem("v_chain")
        a_chain = sem("a_chain")
        b_chain = sem("b_chain")
        b_sub = sem("b_sub")
        b_exp = sem("b_exp")
        choice_made = sem("choice_made")
        ranks_made = sem("ranks_made")
        onehot_made = sem("onehot_made")
        onehot_used = sem("onehot_used")
        table_summed = sem("table_summed")
        table_made = sem("table_made")
        raw_in = [sem(f"raw_in{i}") for i in range(2)]
        w_upper = sem("w_upper")
        w_ready = sem("w_ready")
        row_in = [sem(f"row_in{i}") for i in range(3)]
        rows_turned = sem("rows_turned")
        x_upper = sem("x_upper")
        x_ready = sem("x_ready")
        h_summed = sem("h_summed")
        h_upper = sem("h_upper")
        h_split = sem("h_split")
        y_step = sem("y_step")
        y_tile = sem("y_tile")
        y_taken = sem("y_taken")
        y_ready = sem("y_ready")
        y_added = sem("y_added")
        rows_free = sem("rows_free")
        b2_in = sem("b2_in")
        turn_rows_copied = sem("turn_rows_copied")
        b1_copied = sem("b1_copied")
        weight_copied = sem("weight_copied")

        V, A, G, T = nc.vector, nc.scalar, nc.gpsimd, nc.tensor
        N_CONST = 11
        PAIRS = B // 2
        TURN, GATE, MISC, SCORE, HEAD = 0, 2, 3, 4, 6
        cols_ps = PS[:, MISC, 0:ST * GR].rearrange("p (t g) -> p t g", t=ST)
        logit_ps = PS[:, MISC, 256:256 + ST * E].rearrange("p (t e) -> p t e", t=ST)
        head_ps = PS[:, HEAD:HEAD + 2, :].rearrange("p b (s c) -> p (b s) c", s=2)
        YB, HB, XB = 0, 3, 6

        def small(k, n=ST):
            return sm[:, k, 0:n]

        STEPS = NC * HT
        TURN_AT = {c * HT + 7 + 2 * t: CT * c + t for c in range(NC) for t in range(CT)}
        AHEAD = 2

        def turns_of(n, last):
            m = TURN_AT.get(n)
            return [] if m is None or (last and m >= HI - CT) else [m]

        def x_place(m):
            return (m // CT + 1) % NC, m % CT

        passed = sem("passed")
        from_start = [xn_free, rows_free, head_summed, decay_made, y_taken, turn_copied, gates_taken, cols_copied, scored, head_copied, logits_copied, x1_made, turn_made,
                      cols_made, y_ready]

        def wait_apart(eng, signal, value):
            eng.wait_ge(signal, value)
            eng.sem_inc(passed, 1)

        def wait_step(eng, e, n):
            c, j = divmod(n, HT)
            if j == HT - 1:
                eng.wait_ge(y_tile, e * HI + CT * (c + 1))
            else:
                eng.wait_ge(y_step, e * (NC * (HT - 1)) + (c * (HT - 1) + j + 1))

        def raw_w1(j):
            return raw[:, (j // 2) % 2, 0:2 * D].rearrange("p (k c) -> p k c", k=KT)[:, :, (j % 2) * P:(j % 2 + 1) * P]

        def raw_w2(j):
            return raw[:, (j // 2) % 2, (2 + j % 2) * D:(3 + j % 2) * D]

        block = stack.enter_context(nc.Block())

        @block.sync
        def _(sp):
            sp.wait_ge(pool_const, 1)
            sp.dma_start(wload[0:NH, :], w_fg).then_inc(const_in, 16)
            sp.dma_start(wload[32:32 + NH, :], w_ig).then_inc(const_in, 16)
            sp.dma_start(gate_bias[0:NH, :], b_fg.rearrange("(h o) -> h o", o=1)).then_inc(const_in, 16)
            sp.dma_start(gate_bias[32:32 + NH, :], b_ig.rearrange("(h o) -> h o", o=1)).then_inc(const_in, 16)
            sp.dma_start(rload[:, :], w_router).then_inc(const_in, 16)
            sp.dma_start(bload[:, :], b1.rearrange("e (j p) -> (e j) p", p=P)).then_inc(const_in, 16)
            sp.dma_start(tanh_x[:, :], g_xattn.partition_broadcast(P)).then_inc(const_in, 16)
            sp.dma_start(tanh_f[:, :], g_ffn.partition_broadcast(P)).then_inc(const_in, 16)
            sp.dma_start(gvec[:, :], ln_w.partition_broadcast(P)).then_inc(const_in, 16)
            sp.dma_start(xn_dram[TOK:TOK + PAD, :], zeros[:, :]).then_inc(const_in, 16)
            sp.dma_start(out[TOK:TOK + PAD, :], zeros[:, :]).then_inc(const_in, 16)
            with sp.Fori(0, PAIRS) as i:
                wait_apart(sp, head_summed, START + i * 8)
                for p in range(2):
                    sp.dma_start(xs[p][:, :, :], x_rows[i * 2 + p]).then_inc(batch_in[p], 16)
                    for t in range(ST):
                        sp.dma_start(vs[p][:, t, :, 0:DH], ctx_rows[i * 2 + p, t]).then_inc(batch_in[p], 16)
                for p in range(2):
                    wait_apart(sp, negrow_made, i * 2 + (p + 1))
                    sp.dma_start(negmax_dram[i * 2 + p].rearrange("(h s) -> h s", h=NH), g_neg[:, :]).then_inc(negrow_out, 16)
                    wait_apart(sp, negrow_out, i * 32 + 16 * (p + 1))
                    wait_apart(sp, decay_made, START + i * 8)
                    sp.dma_start(negmax[p][:, :, :].rearrange("q h s -> q (h s)"),
                                 negmax_dram[i * 2 + p].partition_broadcast(P)).then_inc(negmax_in[p], 16)
                for p in range(2):
                    wait_apart(sp, x1_made, START + i * 2 + (p + 1))
                    sp.dma_start(out_rows[i * 2 + p], xs[p][:, :, :]).then_inc(x1_stored, 16)
                    wait_apart(sp, xn_made, i * 2 + (p + 1))
                    sp.dma_start(xn_rows[i * 2 + p], xn[:, :, :]).then_inc(xn_stored, 16)
                wait_apart(sp, x1_stored, i * 32 + 32)
                wait_apart(sp, xn_stored, i * 32 + 32)
                sp.sem_inc(xn_free, 1)

            def load_weights(e, g, wait):
                if wait is not None:
                    wait_apart(sp, w_ready, wait)
                sp.dma_start(raw[:, g % 2, 0:2 * D].rearrange("p (k c) -> p k c", k=KT),
                             w1[e].rearrange("(k p) n -> p k n", p=P)[:, :, 2 * g * P:(2 * g + 2) * P]).then_inc(raw_in[g % 2], 16)
                sp.dma_start(raw[:, g % 2, 2 * D:4 * D].rearrange("p (j n) -> p j n", j=2),
                             w2[e, 2 * g * P:(2 * g + 2) * P, :].rearrange("(j p) n -> p j n", p=P)).then_inc(raw_in[g % 2], 16)

            for g in range(HT // 2):
                load_weights(0, g, None if g < 2 else 2 * (g - 1))

            def load_b2(e):
                wait_apart(sp, y_taken, START + e * HI)
                sp.dma_start(b2_row[:, :], b2[e].partition_broadcast(P)).then_inc(b2_in, 16)

            with sp.Fori(0, E - 1) as e:
                load_b2(e)
                for g in range(HT // 2):
                    load_weights(e + 1, g, e * HT + (HT + 2 * (g - 1)))
            load_b2(E - 1)
            sp.wait_ge(y_added, 16 * HI * E)
            sp.wait_ge(x1_stored, 16 * B)
            sp.wait_ge(xn_stored, 16 * B)
            sp.wait_ge(const_in, 16 * N_CONST)

        @block.gpsimd
        def _(pool):
            for s in from_start:
                pool.sem_inc(s, START)
            G.memset(wload[:, :], 0.0)
            G.memset(zeros[:, :], 0.0).then_inc(pool_const, 1)
            G.memset(ones[:, :], 1.0).then_inc(pool_const, 1)
            pool.wait_ge(pool_const, 2)
            G.affine_select(out=ident[:, :], in_=ones[:, 0:P], compare_op=ALU.is_equal, fill=0.0, base=0,
                            pattern=[[-1, P]], channel_multiplier=1).then_inc(pool_const, 1)
            for p in range(2):
                G.memset(vs[p][:, :, :, DH:VW], 1.0)
            G.affine_select(out=upper[:, :], in_=ones[:, 0:P], compare_op=ALU.is_gt, fill=0.0, base=0,
                            pattern=[[1, P]], channel_multiplier=-1)
            G.memset(g_rows[:, :], 0.0)
            G.iota(iota_e[:, :, :], pattern=[[0, NQ], [-1, E]], base=E, channel_multiplier=0,
                   allow_small_or_imprecise_dtypes=True)
            G.iota(iota_p[:, :], pattern=[[1, P]], base=0, channel_multiplier=0,
                   allow_small_or_imprecise_dtypes=True)
            G.iota(token[:, :].rearrange("p (k t) -> p k t", k=TOPK), pattern=[[0, TOPK], [P, TT]], base=-TOK,
                   channel_multiplier=1, allow_small_or_imprecise_dtypes=True)
            G.iota(pad_row[:, :], pattern=[[0, 1]], base=TOK, channel_multiplier=1,
                   allow_small_or_imprecise_dtypes=True).then_inc(pool_const, 1)
            with pool.Fori(0, PAIRS) as i:
                for n in range(2 * NH):
                    wait_apart(pool, decay_made, START + i * 8 + (n + 1))
                    diag = decay[n % 2][:, :, :].rearrange("p t s -> p (t s)")
                    diag = bass.AP(diag.tensor, diag.offset, [list(diag.ap[0]), [S + P, ST], [1, P]])
                    G.affine_select(out=diag, in_=diag, compare_op=ALU.is_ge, fill=0.0, base=0,
                                    pattern=[[0, ST], [1, P]], channel_multiplier=-1).then_inc(decay_masked, 1)

            pool.wait_ge(table_made, 2)
            pool.wait_ge(xn_stored, 16 * B)
            pool.wait_ge(x1_stored, 16 * B)
            pool.wait_ge(const_in, 16 * N_CONST)

            def gather(rows, ring, free):
                if free is not None:
                    wait_apart(pool, rows_turned, free)
                G.indirect_dma_start(out=gathered[0:RT, ring, :], out_offset=None, in_=xn_dram[:, :],
                                     in_offset=bass.IndirectOffsetOnAxis(ap=rows[0:RT, :], axis=0)
                                     ).then_inc(row_in[ring], 16)

            def add_rows(e, u):
                wait_apart(pool, y_ready, START + e * HI + (u + 1))
                if u > 0:
                    wait_apart(pool, y_added, e * (16 * HI) + 16 * u)
                G.indirect_dma_start(out=out[:, :], out_offset=bass.IndirectOffsetOnAxis(ap=rows_add[u % CT][0:RT, :], axis=0),
                                     in_=y_out[0:RT, u % CT, :], in_offset=None, compute_op=ALU.add,
                                     bounds_check=TOK + PAD - 1, oob_is_err=True).then_inc(y_added, 16)

            for t in range(CT):
                gather(slot_row[:, t:t + 1], t, None)

            def expert(e, last):
                turns = HI - CT if last else HI
                for ring in range(CT):
                    wait_apart(pool, row_in[ring], e * (16 * NC) + 16)
                G.tensor_copy(rows_turn[:, 0:turns], slot_row[:, bass.ds(e * HI + CT, turns)]).then_inc(turn_rows_copied, 1)
                wait_apart(pool, turn_rows_copied, e + 1)
                for c in range(NC):
                    if c < NC - 1 or not last:
                        for m in range(CT * c, CT * c + CT):
                            gather(rows_turn[:, m:m + 1], m % CT, e * HI + (m + 1))
                    for t in range(CT):
                        add_rows(e, CT * c + t)
                wait_apart(pool, y_added, e * (16 * HI) + 16 * HI)
                pool.sem_inc(rows_free, 1)

            with pool.Fori(0, E - 1) as e:
                expert(e, False)
            expert(E - 1, True)

        @block.tensor
        def _(pe):
            pe.wait_ge(const_in, 16 * N_CONST)
            pe.wait_ge(pool_const, 4)
            for k in range(3 * KT):
                T.transpose(PS[:, 0, k * GR:(k + 1) * GR], wload[:, k * P:(k + 1) * P], ident[0:GR, 0:GR])
            for k in range(KT):
                T.transpose(PS[:, 1, k * E:(k + 1) * E], rload[:, k * P:(k + 1) * P], ident[0:E, 0:E])
            T.transpose(PS[:, 2, 0:P], bload[:, :], ident[:, :]).then_inc(weights_turned, 1)
            pe.wait_ge(consts_ready, 1)
            with pe.Fori(0, PAIRS) as i:
                def turn(pos, wide):
                    pe.wait_ge(turn_copied, START + i * 24 + max(pos - 1, 0))
                    for k in range(KT):
                        ins = T.transpose(PS[:, TURN + pos % 2, k * P:(k + 1) * P], wide[k], ident[:, :])
                    ins.then_inc(turn_made, 1)

                for p in range(2):
                    for t in range(ST):
                        pe.wait_ge(q_made, i * 8 + (4 * p + t + 1))
                        turn(8 * p + t, [qn[:, t, k * P:(k + 1) * P] for k in range(KT)])
                    pe.wait_ge(batch_in[p], i * 80 + 80)
                    for t in range(ST):
                        turn(8 * p + 4 + t, [vs[p][:, t, k, 0:DH] for k in range(KT)])
                    pe.wait_ge(turn_copied, START + i * 24 + 8 * (p + 1))
                    pe.wait_ge(gates_taken, START + i * 2 + p)
                    for k in range(2 * KT):
                        src = qT[p][:, k, :] if k < KT else kT[p][:, k - KT, :]
                        ins = T.matmul(PS[0:GR, GATE, :], wgate[:, k, :], src, start=(k == 0), stop=(k == 2 * KT - 1))
                    ins.then_inc(gates_made, 1)
                for p in range(2):
                    wait_apart(pe, gate_rows_made, i * 2 + (p + 1))
                    wait_apart(pe, cols_copied, START + i * 2 + p)
                    for t in range(ST):
                        ins = T.transpose(cols_ps[:, t, :], g_rows[:, t * P:(t + 1) * P], ident[0:GR, 0:GR])
                    ins.then_inc(cols_made, 1)

                def scores(n):
                    p, h = n // NH, n % NH
                    for t in range(ST):
                        pe.wait_ge(scored, START + i * 32 + max(4 * n + t - 1, 0))
                        T.matmul(PS[:, SCORE + t % 2, 0:S - t * P], kT[p][:, h, t * P:(t + 1) * P],
                                 qT[p][:, h, t * P:S], start=True, stop=True).then_inc(scores_made, 1)

                def outputs(n):
                    p, h = n // NH, n % NH
                    pe.wait_ge(head_copied, START + i * 8 + n)
                    for s in range(ST):
                        pe.wait_ge(scored, START + i * 32 + (4 * n + s + 1))
                        for t in range(s + 1):
                            ins = T.matmul(head_ps[:, s, 0:DH + 1], decay[n % 2][:, t, s * P:(s + 1) * P],
                                           vs[p][:, t, h, 0:DH + 1], start=(t == 0), stop=(t == s))
                    ins.then_inc(head_summed, 1)

                scores(0)
                for n in range(2 * NH):
                    if n + 1 < 2 * NH and n + 1 != NH:
                        scores(n + 1)
                    outputs(n)
                    if n + 1 == NH:
                        scores(n + 1)
                for p in range(2):
                    pe.wait_ge(xn_made, i * 2 + (p + 1))
                    for t in range(ST):
                        turn(16 + 4 * p + t, [xn[:, t, k * P:(k + 1) * P] for k in range(KT)])
                    pe.wait_ge(turn_copied, START + i * 24 + (20 + 4 * p))
                    pe.wait_ge(logits_copied, START + i * 2 + p)
                    for t in range(ST):
                        for k in range(KT):
                            ins = T.matmul(logit_ps[:, t, :], kT[p][:, k, t * P:(t + 1) * P], wrouter[:, k, :],
                                           start=(k == 0), stop=(k == KT - 1))
                    ins.then_inc(logits_made, 1)

            pe.wait_ge(choice_made, 1)
            flat = chosen[:, :, :].rearrange("p q e -> p (q e)")
            T.matmul(PS[:, 0, :], upper[:, :], flat, start=True, stop=True)
            T.matmul(PS[:, 1, :], ones[:, 0:P], flat, start=True, stop=True).then_inc(ranks_made, 1)
            for q in range(NQ):
                pe.wait_ge(onehot_made, q + 1)
                T.matmul(PS[:, 2, 0:2 * E * HI], one_lo[:, q % 4, :], hi_vals[:, q % 4, :, :].rearrange("p a h -> p (a h)"),
                         start=(q == 0), stop=(q == NQ - 1)).then_inc(onehot_used, 1)

            def turn_rows(t, bank, landed, copied):
                wait_apart(pe, row_in[t], landed)
                if copied is not None:
                    wait_apart(pe, x_ready, copied)
                for k in range(KT):
                    ins = T.transpose(PS[:, XB + bank, k * P:k * P + RT], gathered[0:RT, t, k * P:(k + 1) * P], ident[0:RT, 0:RT])
                ins.then_inc(rows_turned, 1)

            pe.wait_ge(table_made, 2)
            for t in range(CT):
                turn_rows(t, t % 2, 16, None if t < 2 else t - 1)

            def first_layer(e, n):
                c, j = n // HT % NC, n % HT
                if j == 0:
                    pe.wait_ge(x_ready, e * HI + CT * (n // HT + 1))
                if n // HT % NC == 0:
                    pe.wait_ge(w_ready, e * HT + (n // STEPS * HT + j + 1))
                if n >= 3:
                    pe.wait_ge(h_upper, e * STEPS + (n - 2))
                for k in range(KT):
                    for a, (w, v) in enumerate(((w_hi, x_hi), (w_hi, x_lo), (w_lo, x_hi))):
                        ins = T.matmul(PS[:, HB + n % 3, 0:CW], w[:, j, k * P:(k + 1) * P], v[:, c, k, :],
                                       start=(k == 0 and a == 0), stop=(k == KT - 1 and a == 2))
                ins.then_inc(h_summed, 1)

            def expert(e, last):
                def second_layer(n):
                    c, j = divmod(n, HT)
                    pe.wait_ge(h_split, e * STEPS + (n + 1))
                    for t in range(CT):
                        if j == 0:
                            pe.wait_ge(y_taken, START + e * HI + max(CT * (c - 1) + t + 1, 0))
                        for a, (h, w) in enumerate(((h_hi, w_hi), (h_hi, w_lo), (h_lo, w_hi))):
                            ins = T.matmul(PS[0:RT, YB + t, :], h[:, n % 3, t * RT:(t + 1) * RT], w[:, j, D:2 * D],
                                           start=(j == 0 and a == 0), stop=(j == HT - 1 and a == 2))
                        if j == HT - 1:
                            ins.then_inc(y_tile, 1)
                    if j < HT - 1:
                        ins.then_inc(y_step, 1)

                for n in range(STEPS):
                    if n + AHEAD < STEPS or not last:
                        first_layer(e, n + AHEAD)
                    for m in turns_of(n, last):
                        turn_rows(m % CT, (m + 1) % 2, e * (16 * NC) + 16 * (m // CT + 2), e * HI + (m + 2))
                    second_layer(n)

            for n in range(AHEAD):
                first_layer(0, n)
            with pe.Fori(0, E - 1) as e:
                expert(e, False)
            expert(E - 1, True)

        @block.scalar
        def _(act):
            act.wait_ge(const_in, 16 * N_CONST)
            A.activation(tanh_x[:, :], tanh_x[:, :], ACT.Tanh)
            A.activation(tanh_f[:, :], tanh_f[:, :], ACT.Tanh).then_inc(tanh_made, 1)
            A.preload_act_table_set("natural_log_exp_and_others")
            with act.Fori(0, PAIRS) as i:
                chain = Chain(act, a_chain, i, 8)

                def seed(pos):
                    act.wait_ge(ln_var_made, i * 6 + (pos + 1))
                    chain(A.activation(small(3, ST * NH), small(2, ST * NH), ACT.Ln))
                    A.activation(small(3, ST * NH), small(3, ST * NH), ACT.Exp, scale=-0.5).then_inc(ln_seed_made, 1)

                def copy_turn(pos, dst):
                    act.wait_ge(turn_made, START + i * 24 + (pos + 1))
                    A.copy(dst, PS[:, TURN + pos % 2, :].rearrange("p (k c) -> p k c", k=KT)).then_inc(turn_copied, 1)

                def exponentials(n):
                    p, h = n // NH, n % NH
                    if h == 0:
                        act.wait_ge(cols_copied, START + i * 2 + (p + 1))
                        act.wait_ge(negmax_in[p], i * 16 + 16)
                    act.wait_ge(head_summed, START + i * 8 + max(n - 1, 0))
                    for t in range(ST):
                        ins = A.activation(decay[n % 2][:, t, t * P:S], negmax[p][:, h, t * P:S], ACT.Exp,
                                           bias=cols[p][:, t, h:h + 1])
                    ins.then_inc(decay_made, 1)

                def copy_head(n):
                    act.wait_ge(head_summed, START + i * 8 + (n + 1))
                    if n % NH == 0:
                        act.wait_ge(x1_made, START + i * 2 + n // NH)
                    A.copy(heads[:, :, n % NH, 0:DH + 1], head_ps[:, :, 0:DH + 1]).then_inc(head_copied, 1)

                seed(0)
                seed(1)
                for p in range(2):
                    for t in range(2 * ST):
                        dst = qT[p] if t < ST else kT[p]
                        copy_turn(8 * p + t, dst[:, :, (t % ST) * P:(t % ST + 1) * P])
                for p in range(2):
                    act.wait_ge(abs_made, i * 2 + (p + 1))
                    chain(A.activation(g_t[:, :], g_t[:, :], ACT.Exp, scale=-1.0))
                    A.activation(g_t[:, :], g_t[:, :], ACT.Ln, bias=1.0).then_inc(softplus_made, 1)
                    act.wait_ge(cols_copied, START + i * 2 + (p + 1))
                    A.activation(expneg[p][:, :, :], cols[p][:, :, 32:32 + NH], ACT.Exp).then_inc(expneg_made, 1)
                for n in range(2 * NH):
                    exponentials(n)
                    if n > 0:
                        copy_head(n - 1)
                    if n == NH:
                        seed(2)
                        seed(3)
                copy_head(2 * NH - 1)
                for t in range(ST):
                    copy_turn(16 + t, kT[0][:, :, t * P:(t + 1) * P])
                seed(4)
                seed(5)
                for t in range(ST):
                    copy_turn(20 + t, kT[1][:, :, t * P:(t + 1) * P])
                assert chain.n == 8, chain.n
            act.wait_ge(b_sub, 1)
            A.activation(prob[:, :, :], prob[:, :, :], ACT.Exp).then_inc(b_exp, 1)

            def upper_x(c, t, bank, turned):
                act.wait_ge(rows_turned, turned)
                A.copy(x_hi[:, c, :, t * RT:(t + 1) * RT],
                       PS[:, XB + bank, :].rearrange("p (k c) -> p k c", k=KT)[:, :, 0:RT]).then_inc(x_upper, 1)

            def upper_w(j, raw_arrived, free=None):
                g, jj = j // 2, j % 2
                if jj == 0:
                    act.wait_ge(raw_in[g % 2], raw_arrived)
                if free is not None:
                    wait_step(act, *free)
                A.copy(w_hi[:, j, 0:D].rearrange("p (k c) -> p k c", k=KT), raw_w1(j))
                A.copy(w_hi[:, j, D:2 * D], raw_w2(j)).then_inc(w_upper, 1)

            act.wait_ge(table_made, 2)
            for t in range(CT):
                upper_x(0, t, t % 2, t + 1)
            act.wait_ge(x1_stored, 16 * B)
            act.wait_ge(xn_stored, 16 * B)
            for j in range(HT):
                upper_w(j, 32 * (j // 4 + 1))

            def hidden(e, n):
                if n % STEPS == 0:
                    if n > 0:
                        act.wait_ge(h_upper, e * STEPS + n)
                    A.copy(b1_now[:, :], b1_all[:, bass.ds(e * HT + n // STEPS * HT, HT)]).then_inc(b1_copied, 1)
                    act.wait_ge(b1_copied, e + (n // STEPS + 1))
                act.wait_ge(h_summed, e * STEPS + (n + 1))
                if n >= 3:
                    act.wait_ge(h_split, e * STEPS + (n - 2))
                A.activation(h_raw[:, n % 3, :], PS[:, HB + n % 3, 0:CW], ACT.Gelu, bias=b1_now[:, n % HT:n % HT + 1])
                A.activation(h_hi[:, n % 3, :], PS[:, HB + n % 3, 0:CW], ACT.Gelu,
                             bias=b1_now[:, n % HT:n % HT + 1]).then_inc(h_upper, 1)

            def expert(e, last):
                def next_w(j):
                    upper_w(j, e * 128 + (128 + 32 * (j // 4 + 1)), (e, STEPS - HT + j))

                for n in range(AHEAD, STEPS if last else STEPS + AHEAD):
                    hidden(e, n)
                    for m in turns_of(n - AHEAD, last):
                        upper_x(*x_place(m), (m + 1) % 2, e * HI + (CT + m + 1))
                    if not last and n >= STEPS - HT + 3:
                        next_w(n - (STEPS - HT + 3))
                if not last:
                    next_w(HT - 1)

            for n in range(AHEAD):
                hidden(0, n)
            with act.Fori(0, E - 1) as e:
                expert(e, False)
            expert(E - 1, True)

        @block.vector
        def _(dve):
            link = Chain(dve, v_setup)
            dve.wait_ge(weights_turned, 1)
            wt = PS[:, 0, 0:3 * KT * GR].rearrange("p (k g) -> p k g", g=GR)
            link(V.tensor_copy(wgate[:, :, :], wt[:, 0:2 * KT, :]))
            link(V.tensor_tensor(wgate[:, KT:2 * KT, :], wgate[:, KT:2 * KT, :], wt[:, 2 * KT:3 * KT, :], ALU.add))
            link(V.tensor_copy(wrouter[:, :, :], PS[:, 1, 0:KT * E].rearrange("p (k e) -> p k e", e=E)))
            link(V.tensor_copy(b1_all[:, :], PS[:, 2, 0:P]))
            dve.wait_ge(tanh_made, 1)
            link(V.tensor_scalar(gvec[:, :], gvec[:, :], 1.0, tanh_x[:, 0:1], ALU.add, ALU.mult))
            V.memset(sm[:, :, :], 1.0).then_inc(consts_ready, 1)
            dve.wait_ge(consts_ready, 1)

            V_TURN = 66
            with dve.Fori(0, PAIRS) as i:
                chain = Chain(dve, v_chain, i, V_TURN)

                def inverse_root(pos, n):
                    dve.wait_ge(ln_seed_made, i * 6 + (pos + 1))
                    chain(V.tensor_tensor(small(4, n), small(3, n), small(2, n), ALU.mult))
                    chain(V.tensor_tensor(small(4, n), small(4, n), small(3, n), ALU.mult))
                    chain(V.tensor_scalar(small(4, n), small(4, n), -0.5, 1.5, ALU.mult, ALU.add))
                    chain(V.tensor_tensor(small(3, n), small(3, n), small(4, n), ALU.mult))

                mv = sm[:, 0:2, 0:ST].rearrange("p a t -> p t a")

                def layer_norm(src, dst, pos, signal, ready):
                    for t in range(ST):
                        ins = V.bn_stats(st6[:, t, :], src[:, t, :])
                    chain(ins)
                    dve.sem_inc(passed, 1)
                    for t in range(ST):
                        ins = V.bn_aggr(mv[:, t, :], st6[:, t, :])
                    chain(ins)
                    V.tensor_scalar(small(2), small(1), LN_EPS, None, ALU.add).then_inc(ln_var_made, 1)
                    inverse_root(pos, ST)
                    ready()
                    for t in range(ST):
                        ins = V.tensor_scalar(dst[:, t, :], src[:, t, :], sm[:, 0, t:t + 1], sm[:, 3, t:t + 1], ALU.subtract, ALU.mult)
                        if signal is q_made:
                            ins.then_inc(q_made, 1)
                    if signal is not q_made:
                        ins.then_inc(signal, 1)

                for p in range(2):
                    dve.wait_ge(batch_in[p], i * 80 + 80)
                    layer_norm(xs[p], qn, p, q_made, lambda: dve.wait_ge(turn_made, START + i * 24 + 4 * p))
                    dve.wait_ge(q_made, i * 8 + 4 * (p + 1))

                for p in range(2):
                    dve.wait_ge(gates_made, i * 2 + (p + 1))
                    gates = PS[:, GATE, :]
                    V.tensor_scalar(g_f[:, :], gates[0:NH, :], gate_bias[0:NH, 0:1], None, ALU.add)
                    chain(V.tensor_scalar(g_i[:, :], gates[32:32 + NH, :], gate_bias[32:32 + NH, 0:1], None, ALU.add))
                    V.scalar_tensor_tensor(g_t[:, :], g_f[:, :], -1.0, g_f[:, :], ALU.mult, ALU.max).then_inc(abs_made, 1)
                    dve.sem_inc(gates_taken, 1)
                    dve.wait_ge(softplus_made, i * 2 + (p + 1))
                    chain(V.scalar_tensor_tensor(g_f[:, :], g_f[:, :], 0.0, g_t[:, :], ALU.min, ALU.subtract))
                    chain(V.tensor_tensor_scan(g_cum[:, :], ones[0:NH, :], g_f[:, :], 0.0, ALU.mult, ALU.add))
                    chain(V.tensor_tensor(g_i[:, :], g_i[:, :], g_cum[:, :], ALU.subtract))
                    chain(V.tensor_tensor_scan(g_max[:, :], ones[0:NH, :], g_i[:, :], LOWEST, ALU.mult, ALU.max))
                    if p == 1:
                        dve.wait_ge(negrow_out, i * 32 + 16)
                    dve.wait_ge(cols_made, START + i * 2 + p)
                    V.tensor_scalar(g_neg[:, :], g_max[:, :], -1.0, None, ALU.mult).then_inc(negrow_made, 1)
                    V.tensor_copy(g_rows[0:NH, :], g_i[:, :])
                    V.scalar_tensor_tensor(g_rows[32:32 + NH, :], g_cum[:, :], -1.0, g_max[:, :], ALU.mult, ALU.subtract)\
                        .then_inc(gate_rows_made, 1)
                    dve.wait_ge(cols_made, START + i * 2 + (p + 1))
                    V.tensor_copy(cols[p][:, :, :], cols_ps).then_inc(cols_copied, 1)

                def weigh(n):
                    dve.wait_ge(decay_masked, i * 8 + (n + 1))
                    for t in range(ST):
                        dve.wait_ge(scores_made, i * 32 + (4 * n + t + 1))
                        d = decay[n % 2][:, t, t * P:S]
                        V.scalar_tensor_tensor(d, PS[:, SCORE + t % 2, 0:S - t * P], SCORE_SCALE, d, ALU.mult, ALU.mult)\
                            .then_inc(scored, 1)

                def finish(p):
                    n = ST * NH
                    dve.wait_ge(head_copied, START + i * 8 + 4 * (p + 1))
                    for t in range(ST):
                        for h in range(NH):
                            ins = V.bn_stats(st6[:, t * NH + h, :], heads[:, t, h, 0:DH])
                    chain(ins)
                    dve.wait_ge(expneg_made, i * 2 + (p + 1))
                    sums = heads[:, :, :, DH]
                    r = small(5, n).rearrange("p (t h) -> p t h", t=ST)
                    chain(V.scalar_tensor_tensor(r, sums, -1.0, sums, ALU.mult, ALU.max))
                    chain(V.tensor_tensor(r, r, expneg[p][:, :, :], ALU.max))
                    chain(V.tensor_scalar(small(5, n), small(5, n), NORM_EPS, None, ALU.add))
                    V.reciprocal(small(5, n), small(5, n))
                    V.tensor_tensor(small(6, n), st6[:, :, 1], st6[:, :, 4], ALU.add)
                    V.tensor_tensor(small(7, n), st6[:, :, 1], st6[:, :, 4], ALU.subtract)
                    chain(V.tensor_tensor(small(8, n), st6[:, :, 2], st6[:, :, 5], ALU.add))
                    V.tensor_scalar(small(6, n), small(6, n), 0.5, None, ALU.mult)
                    chain(V.scalar_tensor_tensor(small(7, n), small(7, n), 0.25, small(7, n), ALU.mult, ALU.mult))
                    chain(V.scalar_tensor_tensor(small(7, n), small(8, n), 1.0 / DH, small(7, n), ALU.mult, ALU.add))
                    chain(V.tensor_tensor(small(7, n), small(7, n), small(5, n), ALU.mult))
                    chain(V.tensor_tensor(small(7, n), small(7, n), small(5, n), ALU.mult))
                    V.tensor_scalar(small(2, n), small(7, n), LN_EPS, None, ALU.add).then_inc(ln_var_made, 1)
                    inverse_root(2 + 2 * p, n)
                    chain(V.tensor_tensor(small(9, n), small(3, n), small(5, n), ALU.mult))
                    for t in range(ST):
                        for h in range(NH):
                            k = t * NH + h
                            ins = V.tensor_scalar(heads[:, t, h, 0:DH], heads[:, t, h, 0:DH], sm[:, 6, k:k + 1], sm[:, 9, k:k + 1],
                                                  ALU.subtract, ALU.mult)
                    chain(ins)
                    dve.wait_ge(turn_made, START + i * 24 + 20 * p)
                    if p == 0:
                        dve.wait_ge(xn_free, START + i)
                    else:
                        dve.wait_ge(xn_stored, i * 32 + 16)
                    for t in range(ST):
                        ins = V.tensor_tensor(xn[:, t, :].rearrange("p (h c) -> p h c", h=NH), heads[:, t, :, 0:DH],
                                              gvec[:, :].rearrange("p (h c) -> p h c", h=NH), ALU.mult)
                    chain(ins)
                    for t in range(ST):
                        ins = V.tensor_tensor(xs[p][:, t, :], xs[p][:, t, :], xn[:, t, :], ALU.add)
                    ins.then_inc(x1_made, 1)
                    dve.wait_ge(x1_made, START + i * 2 + (p + 1))
                    layer_norm(xs[p], xn, 3 + 2 * p, xn_made, lambda: None)

                for n in range(NH):
                    weigh(n)
                finish(0)
                for n in range(NH, 2 * NH):
                    weigh(n)
                finish(1)
                for p in range(2):
                    dve.wait_ge(logits_made, i * 2 + (p + 1))
                    V.tensor_copy(logits[:, bass.ds(i * 8 + 4 * p, ST), :], logit_ps).then_inc(logits_copied, 1)
                dve.wait_ge(negrow_out, i * 32 + 32)
                assert chain.n == V_TURN, ("V_TURN", chain.n)

            link = Chain(dve, b_chain)
            top = rb[:, 0, :]
            dve.wait_ge(logits_copied, START + B)

            def over_e(v, n):
                return v.rearrange("p (q o) -> p q o", o=1).to_broadcast([P, n, E])

            link(V.tensor_reduce(rb[:, 1, 0:TT], logits[:, :, :], AX.X, ALU.max))
            V.tensor_tensor(prob[:, :, :], logits[:, :, :], over_e(rb[:, 1, 0:TT], TT), ALU.subtract).then_inc(b_sub, 1)
            dve.wait_ge(b_exp, 1)
            link(V.tensor_reduce(rb[:, 1, 0:TT], prob[:, :, :], AX.X, ALU.add))
            link(V.reciprocal(rb[:, 1, 0:TT], rb[:, 1, 0:TT]))
            link(V.tensor_tensor(prob[:, :, :], prob[:, :, :], over_e(rb[:, 1, 0:TT], TT), ALU.mult))
            for k in range(TOPK):
                q0, q1 = k * TT, (k + 1) * TT
                first = iota_e[:, q0:q1, :]
                link(V.tensor_reduce(top[:, q0:q1], prob[:, :, :], AX.X, ALU.max))
                link(V.tensor_tensor(work[:, q0:q1, :], prob[:, :, :], over_e(top[:, q0:q1], TT), ALU.is_equal))
                link(V.tensor_tensor(work[:, q0:q1, :], work[:, q0:q1, :], first, ALU.mult))
                link(V.tensor_reduce(rb[:, 2, q0:q1], work[:, q0:q1, :], AX.X, ALU.max))
                link(V.tensor_tensor(chosen[:, q0:q1, :], first, over_e(rb[:, 2, q0:q1], TT), ALU.is_equal))
                if k == 0:
                    link(V.scalar_tensor_tensor(prob[:, :, :], chosen[:, q0:q1, :], -2.0, prob[:, :, :], ALU.mult, ALU.add))
            dve.sem_inc(choice_made, 1)
            dve.wait_ge(ranks_made, 1)
            link(V.tensor_copy(work[:, :, :], PS[:, 1, :].rearrange("p (q e) -> p q e", e=E)))
            for ex in range(E):
                ins = V.tensor_tensor_scan(base[:, :, ex], ones[:, 0:NQ], work[:, :, ex], 0.0, ALU.mult, ALU.add)
            link(ins)
            link(V.tensor_tensor(base[:, :, :], base[:, :, :], work[:, :, :], ALU.subtract))
            link(V.tensor_tensor(base[:, :, :], base[:, :, :], PS[:, 0, :].rearrange("p (q e) -> p q e", e=E), ALU.add))
            link(V.tensor_tensor(base[:, :, :], base[:, :, :], chosen[:, :, :], ALU.mult))
            link(V.tensor_reduce(rb[:, 3, :], base[:, :, :], AX.X, ALU.add))
            link(V.tensor_scalar(rb[:, 4, :], rb[:, 3, :], 1.0 / RT, 0.5 / RT - 0.5, ALU.mult, ALU.add))
            link(V.tensor_scalar(rb[:, 4, :], rb[:, 4, :], ROUND, None, ALU.add))
            link(V.tensor_scalar(rb[:, 4, :], rb[:, 4, :], -ROUND, None, ALU.add))
            link(V.scalar_tensor_tensor(rb[:, 5, :], rb[:, 4, :], -float(RT), rb[:, 3, :], ALU.mult, ALU.add))
            link(V.tensor_scalar(rb[:, 2, :], rb[:, 2, :], -float(HI), float(E * HI), ALU.mult, ALU.add))
            link(V.tensor_tensor(rb[:, 4, :], rb[:, 4, :], rb[:, 2, :], ALU.add))
            link(V.tensor_scalar(rb[:, 3, :], rb[:, 3, :], float(CAP), DROPPED, ALU.is_ge, ALU.mult))
            link(V.tensor_tensor(rb[:, 4, :], rb[:, 4, :], rb[:, 3, :], ALU.add))
            V.tensor_tensor(rb[:, 6, :], token[:, :], rb[:, 5, :], ALU.subtract)
            link(V.tensor_scalar(rb[:, 7, :], top, tanh_f[:, 0:1], None, ALU.mult))
            for q in range(NQ):
                if q >= 4:
                    dve.wait_ge(onehot_used, q - 3)
                V.tensor_scalar(one_lo[:, q % 4, :], iota_p[:, :], rb[:, 5, q:q + 1], None, ALU.is_equal)
                for a in range(2):
                    ins = V.tensor_scalar(hi_vals[:, q % 4, a, :], iota_p[:, 0:E * HI], rb[:, 4, q:q + 1], rb[:, 6 + a, q:q + 1],
                                          ALU.is_equal, ALU.mult)
                ins.then_inc(onehot_made, 1)
            dve.wait_ge(onehot_used, NQ)
            link(V.tensor_scalar(row_f[:, :], PS[:, 2, 0:E * HI], pad_row[:, 0:1], None, ALU.add))
            V.tensor_copy(slot_row[:, :], row_f[:, :]).then_inc(table_made, 1)
            V.tensor_copy(slot_weight[:, :], PS[:, 2, E * HI:2 * E * HI]).then_inc(table_made, 1)
            dve.wait_ge(table_made, 2)

            def rest_of_w(j, count):
                dve.wait_ge(w_upper, count)
                V.tensor_tensor(w_lo[:, j, 0:D].rearrange("p (k c) -> p k c", k=KT), raw_w1(j),
                                w_hi[:, j, 0:D].bitcast(F32).rearrange("p (k c) -> p k c", k=KT), ALU.subtract)
                V.tensor_tensor(w_lo[:, j, D:2 * D], raw_w2(j), w_hi[:, j, D:2 * D].bitcast(F32), ALU.subtract)\
                    .then_inc(w_ready, 1)

            def rest_of_x(c, t, bank, count):
                dve.wait_ge(x_upper, count)
                V.tensor_tensor(x_lo[:, c, :, t * RT:(t + 1) * RT], PS[:, XB + bank, :].rearrange("p (k c) -> p k c", k=KT)[:, :, 0:RT],
                                x_hi[:, c, :, t * RT:(t + 1) * RT].bitcast(F32), ALU.subtract).then_inc(x_ready, 1)

            dve.wait_ge(x1_stored, 16 * B)
            dve.wait_ge(xn_stored, 16 * B)
            for t in range(CT):
                rest_of_x(0, t, t % 2, t + 1)
            for j in range(HT):
                rest_of_w(j, j + 1)

            def split_hidden(e, n):
                dve.wait_ge(h_upper, e * STEPS + (n + 1))
                V.tensor_tensor(h_lo[:, n % 3, :], h_raw[:, n % 3, :], h_hi[:, n % 3, :].bitcast(F32), ALU.subtract)\
                    .then_inc(h_split, 1)

            def expert(e, last):
                dve.wait_ge(y_ready, START + e * HI)
                V.tensor_copy(weight_now[:, :], slot_weight[:, bass.ds(e * HI, HI)]).then_inc(weight_copied, 1)
                dve.wait_ge(weight_copied, e + 1)

                def take(c):
                    for t in range(CT):
                        u = CT * c + t
                        dve.wait_ge(y_tile, e * HI + (u + 1))
                        if u == 0:
                            dve.wait_ge(b2_in, e * 16 + 16)
                        if c == 0:
                            dve.wait_ge(rows_free, START + e)
                        else:
                            dve.wait_ge(y_added, e * (16 * HI) + 16 * (u - CT + 1))
                        V.tensor_tensor(y_out[0:RT, t, :], PS[0:RT, YB + t, :], b2_row[0:RT, :], ALU.add).then_inc(y_taken, 1)

                def weigh_rows(c):
                    for t in range(CT):
                        u = CT * c + t
                        V.tensor_copy(rows_add[t][:, :], slot_row[:, bass.ds(e * HI + u, 1)])
                        dve.wait_ge(y_taken, START + e * HI + (u + 1))
                        V.tensor_scalar(y_out[0:RT, t, :], y_out[0:RT, t, :], weight_now[0:RT, u:u + 1], None,
                                        ALU.mult).then_inc(y_ready, 1)

                def next_w(j):
                    rest_of_w(j, e * HT + (HT + j + 1))

                for n in range(AHEAD, STEPS if last else STEPS + AHEAD):
                    split_hidden(e, n)
                    for m in turns_of(n - AHEAD, last):
                        rest_of_x(*x_place(m), (m + 1) % 2, e * HI + (CT + m + 1))
                    if not last and n >= STEPS - HT + 3:
                        next_w(n - (STEPS - HT + 3))
                    if n > HT and n % HT == AHEAD - 1:
                        take(n // HT - 1)
                        if n > STEPS:
                            next_w(HT - 1)
                        weigh_rows(n // HT - 1)
                if last:
                    take(NC - 1)
                    weigh_rows(NC - 1)

            for n in range(AHEAD):
                split_hidden(0, n)
            with dve.Fori(0, E - 1) as e:
                expert(e, False)
            expert(E - 1, True)


_INS = ['x', 'ctx_1024', 'g_xattn', 'g_ffn', 'L0_xattn_w_igate', 'L0_xattn_b_igate', 'L0_xattn_w_fgate',
        'L0_xattn_b_fgate', 'L0_xattn_ln_weight', 'L0_ffn_Wg', 'L0_ffn_W1', 'L0_ffn_b1', 'L0_ffn_W2', 'L0_ffn_b2']


def kernel(**inputs):
    import numpy as _np
    import concourse.bacc as _bacc
    from concourse import mybir as _mybir
    from concourse.bass_utils import run_bass_kernel_spmd as _run

    nc = _bacc.Bacc("TRN2", target_bir_lowering=False, num_devices=1)
    arrays, args = {}, []
    for name in _INS:
        a = _np.ascontiguousarray(inputs[name])
        arrays[f"in_{name}_dram"] = a
        args.append(nc.dram_tensor(f"in_{name}_dram", a.shape, _mybir.dt.from_np(a.dtype), kind="ExternalInput").ap())
    args.append(nc.dram_tensor("out_0_dram", (TOK + PAD, D), _mybir.dt.float32, kind="ExternalOutput").ap())
    build(nc, *args)
    r = _run(nc, [arrays], core_ids=[0])
    return r.results[0]["out_0_dram"][0:TOK].reshape(B, S, D)
```

```python
from contextlib import ExitStack

import concourse.bass as bass
from concourse import mybir

F32 = mybir.dt.float32
F32R = mybir.dt.float32r
I32 = mybir.dt.int32
ALU = mybir.AluOpType
ACT = mybir.ActivationFunctionType
AX = mybir.AxisListType

P = 128
B, S, D = 8, 512, 512
NH = 4
DH = D // NH
ST = S // P
KT = D // P
E = 8
HID = 2048
HT = HID // P
TOK = B * S
TT = TOK // P
TOPK = 2
CAP = int(round(TOPK * TOK * 1.05 / E))
HI = -(-CAP // P)
RT = 2 * -(-CAP // (2 * HI))
CT = 3
NC = HI // CT
CW = CT * RT
assert HI == CT * NC and CW <= 512 and CAP <= HI * RT
PAD = P
NQ = TOPK * TT
LN_EPS = 1e-5
NORM_EPS = 1e-6
SCORE_SCALE = float(DH) ** -0.5
VW = DH + 2
GR = 36
DROPPED = 1000.0
LOWEST = -3.0e38
QG = 8
ROUND = 1.5 * 2 ** 23
START = 3


class Chain:

    def __init__(self, engine, signal, turn=0, per_turn=0):
        self.engine, self.sem, self.turn, self.per_turn, self.n = engine, signal, turn, per_turn, 0

    def __call__(self, ins):
        self.n += 1
        ins.then_inc(self.sem, 1)
        self.engine.wait_ge(self.sem, self.turn * self.per_turn + self.n)

    def closed(self):
        assert self.n == self.per_turn, (self.sem, self.n)


def build(nc, x, ctx_in, g_xattn, g_ffn, w_ig, b_ig, w_fg, b_fg, ln_w, w_router, w1, b1, w2, b2, out):
    x_rows = x.rearrange("b (t p) d -> b p t d", p=P)
    ctx_rows = ctx_in.rearrange("b (t p) (h c) -> b t p h c", p=P, h=NH)
    xn_dram = nc.dram_tensor("xn_rows", (TOK + PAD, D), F32, kind="Internal").ap()
    negmax_dram = nc.dram_tensor("negmax_rows", (B, NH * S), F32, kind="Internal").ap()
    out_rows = out[0:TOK, :].rearrange("(b t p) d -> b p t d", b=B, p=P)
    xn_rows = xn_dram[0:TOK, :].rearrange("(b t p) d -> b p t d", b=B, p=P)

    stack = ExitStack()
    with stack:
        def sb(name, shape, dt=F32, where=stack):
            return where.enter_context(nc.sbuf_tensor(name, shape, dt))

        def sem(name):
            return stack.enter_context(nc.semaphore(name))

        PS = stack.enter_context(nc.psum_tensor("PS", [P, 8, 512], F32))

        ident = sb("ident", [P, P])
        b1_all = sb("b1_all", [P, E * HT])
        slot_row = sb("slot_row", [P, E * HI], I32)
        slot_weight = sb("slot_weight", [P, E * HI])

        a_mem = ExitStack()
        ones = sb("ones", [P, S], F32, a_mem)
        logits = sb("logits", [P, TT, E], F32, a_mem)
        tanh_f = sb("tanh_f", [P, 1], F32, a_mem)
        iota_e = sb("iota_e", [P, NQ, E], F32, a_mem)
        iota_p = sb("iota_p", [P, P], F32, a_mem)
        token = sb("token", [P, NQ], F32, a_mem)
        upper = sb("upper", [P, P], F32, a_mem)
        pad_row = sb("pad_row", [P, 1], F32, a_mem)
        prob = sb("prob", [P, TT, E], F32, a_mem)
        work = sb("work", [P, NQ, E], F32, a_mem)
        chosen = sb("chosen", [P, NQ, E], F32, a_mem)
        base = sb("base", [P, NQ, E], F32, a_mem)
        rb = sb("rb", [P, 8, NQ], F32, a_mem)
        row_f = sb("row_f", [P, E * HI], F32, a_mem)
        b_mem = a_mem.enter_context(ExitStack())
        one_lo = sb("one_lo", [P, 2, QG, P], F32, b_mem)
        one_hi = sb("one_hi", [P, 2, QG, E * HI], F32, b_mem)
        hi_vals = sb("hi_vals", [P, 2, QG, 2, E * HI], F32, b_mem)
        b_mem.close()
        zeros = sb("zeros", [P, D], F32, a_mem)
        gate_bias = sb("gate_bias", [GR, 1], F32, a_mem)
        tanh_x = sb("tanh_x", [P, 1], F32, a_mem)
        wrouter = sb("wrouter", [P, KT, E], F32, a_mem)
        wgate = sb("wgate", [P, 2 * KT, GR], F32, a_mem)
        gvec = sb("gvec", [P, D], F32, a_mem)
        g_f = sb("g_f", [NH, S], F32, a_mem)
        g_i = sb("g_i", [NH, S], F32, a_mem)
        g_t = sb("g_t", [NH, S], F32, a_mem)
        g_cum = sb("g_cum", [NH, S], F32, a_mem)
        g_max = sb("g_max", [NH, S], F32, a_mem)
        g_rows = sb("g_rows", [GR, S], F32, a_mem)
        g_neg = sb("g_neg", [NH, S], F32, a_mem)
        logit_rows = sb("logit_rows", [E, S], F32, a_mem)
        cols = [sb(f"cols{p}", [P, ST, GR], F32, a_mem) for p in range(2)]
        expneg = [sb(f"expneg{p}", [P, ST, NH], F32, a_mem) for p in range(2)]
        stats = [sb(f"stats{k}", [P, (ST, ST * NH, ST)[k], 6], F32, a_mem) for k in range(3)]
        small = [sb(f"small{k}", [P, 10, ST * NH], F32, a_mem) for k in range(3)]
        heads = [sb(f"heads{p}", [P, ST, NH, VW], F32, a_mem) for p in range(2)]
        x_back = sb("x_back", [P, ST, D], F32, a_mem)
        xn = sb("xn", [P, ST, D], F32, a_mem)
        xnT = sb("xnT", [P, KT, S], F32, a_mem)
        x_front = sb("x_front", [P, ST, D], F32, a_mem)
        qn = sb("qn", [P, ST, D], F32, a_mem)
        vs = [sb(f"vs{p}", [P, ST, NH, VW], F32, a_mem) for p in range(2)]
        setup_mem = a_mem.enter_context(ExitStack())
        wload = sb("wload", [GR, 3 * D], F32, setup_mem)
        rload = sb("rload", [E, D], F32, setup_mem)
        bload = sb("bload", [E * HT, P], F32, setup_mem)
        setup_mem.close()
        qT = [sb(f"qT{p}", [P, KT, S], F32, a_mem) for p in range(2)]
        kT = [sb(f"kT{p}", [P, KT, S], F32, a_mem) for p in range(2)]
        decay = [sb(f"decay{p}", [P, ST, S], F32, a_mem) for p in range(2)]
        negmax = [sb(f"negmax{p}", [P, NH, S], F32, a_mem) for p in range(2)]
        a_mem.close()

        x_hi = sb("x_hi", [P, NC, KT, CW], F32R)
        x_lo = sb("x_lo", [P, NC, KT, CW], F32R)
        h_raw = sb("h_raw", [P, 3, CW])
        h_hi = sb("h_hi", [P, 3, CW], F32R)
        h_lo = sb("h_lo", [P, 3, CW], F32R)
        y_out = sb("y_out", [P, CT, D])
        b2_row = sb("b2_row", [P, D])
        b1_now = sb("b1_now", [P, HT])
        weight_now = sb("weight_now", [P, HI])
        rows_add = [sb(f"rows_add{t}", [P, 1], I32) for t in range(CT)]
        rows_turn = sb("rows_turn", [P, HI], I32)
        w_hi = sb("w_hi", [P, HT, 2 * D], F32R)
        w_lo = sb("w_lo", [P, HT, 2 * D], F32R)
        raw = sb("raw", [P, 2, 4 * D])
        gathered = sb("gathered", [P, 3, D])

        const_in = sem("const_in")
        pool_const = sem("pool_const")
        weights_turned = sem("weights_turned")
        consts_ready = sem("consts_ready")
        tanh_made = sem("tanh_made")
        v_setup = sem("v_setup")
        x_front_in = sem("x_front_in")
        x_back_in = sem("x_back_in")
        ctx_in_sb = [sem(f"ctx_in_sb{p}") for p in range(2)]
        var_made = [sem(f"var_made{k}") for k in range(3)]
        seed_made = [sem(f"seed_made{k}") for k in range(3)]
        q_made = sem("q_made")
        front_turned = sem("front_turned")
        front_copied = sem("front_copied")
        back_turned = sem("back_turned")
        back_copied = sem("back_copied")
        gates_made = sem("gates_made")
        gates_taken = sem("gates_taken")
        abs_made = sem("abs_made")
        softplus_made = sem("softplus_made")
        negrow_made = sem("negrow_made")
        negrow_out = sem("negrow_out")
        negmax_in = [sem(f"negmax_in{p}") for p in range(2)]
        gate_rows_made = sem("gate_rows_made")
        cols_made = sem("cols_made")
        cols_copied = sem("cols_copied")
        expneg_made = sem("expneg_made")
        decay_made = sem("decay_made")
        decay_masked = sem("decay_masked")
        scores_made = sem("scores_made")
        scored = sem("scored")
        head_summed = sem("head_summed")
        head_copied = sem("head_copied")
        heads_normed = sem("heads_normed")
        heads_weighed = sem("heads_weighed")
        x1_made = sem("x1_made")
        xn_made = sem("xn_made")
        x1_stored = sem("x1_stored")
        xn_stored = sem("xn_stored")
        router_summed = sem("router_summed")
        router_copied = sem("router_copied")
        logits_made = sem("logits_made")
        logits_copied = sem("logits_copied")
        v_chain = sem("v_chain")
        a_chain = sem("a_chain")
        a_setup = sem("a_setup")
        b_chain = sem("b_chain")
        b_sub = sem("b_sub")
        b_exp = sem("b_exp")
        choice_made = sem("choice_made")
        ranks_made = sem("ranks_made")
        one_hi_made = sem("one_hi_made")
        rows_spread = sem("rows_spread")
        onehot_made = sem("onehot_made")
        onehot_used = sem("onehot_used")
        table_made = sem("table_made")
        raw_in = [sem(f"raw_in{i}") for i in range(2)]
        w_upper = sem("w_upper")
        w_ready = sem("w_ready")
        row_in = [sem(f"row_in{i}") for i in range(3)]
        rows_turned = sem("rows_turned")
        x_upper = sem("x_upper")
        x_ready = sem("x_ready")
        h_summed = sem("h_summed")
        h_upper = sem("h_upper")
        h_split = sem("h_split")
        y_step = sem("y_step")
        y_tile = sem("y_tile")
        y_taken = sem("y_taken")
        y_ready = sem("y_ready")
        y_added = sem("y_added")
        rows_free = sem("rows_free")
        b2_in = sem("b2_in")
        turn_rows_copied = sem("turn_rows_copied")
        b1_copied = sem("b1_copied")
        weight_copied = sem("weight_copied")

        V, A, G, T = nc.vector, nc.scalar, nc.gpsimd, nc.tensor
        N_CONST = 9
        TURN, GATE, SCORE, HEAD = 0, 2, 3, 6
        places = PS[:, HEAD:HEAD + 2, :].rearrange("p b (s c) -> p (b s) c", s=2)
        head_ps = places[:, :, 0:VW]
        cols_ps = PS[:, GATE, 0:ST * GR].rearrange("p (t g) -> p t g", t=ST)
        logit_ps = PS[:, TURN + 1, 0:ST * E].rearrange("p (t e) -> p t e", t=ST)

        def back_ps(t, spread):
            return PS[:, (GATE, SCORE, SCORE + 1, SCORE + 2)[t] if spread else GATE, :]

        SCORE_ORDER = [0, 1, 3, 2]
        MADE = [1, 3, 3, 4]
        READ = [-3, -1, -1, 0]
        NEEDED = [1, 2, 4, 4]
        score_ps = [PS[:, SCORE, 0:S], PS[:, SCORE + 1, 0:S - P], PS[:, SCORE + 2, 0:S - 2 * P],
                    PS[:, SCORE + 1, S - P:S]]

        def near(b, step):
            return (b[0], b[1] + step)

        def at(b, each, more):
            return b[0] * (2 * each) + (b[1] * each + more)

        def at_own(b, each, more):
            return b[0] * each + (b[1] // 2 * each + more)

        def number(b):
            return b[0] * 2 + b[1]

        EARLY, MIDDLE = range(0, HT // 2), range(HT // 2, HT - 4)
        LATE = range(HT - 4, HT)
        LAST_BATCH = (0, B - 1)

        def one_hot(out, width, which):
            return nc.vector.tensor_tensor(out, iota_p[:, 0:width].rearrange("p (o c) -> p o c", o=1).to_broadcast([P, QG, width]),
                                           which.rearrange("p (q o) -> p q o", o=1).to_broadcast([P, QG, width]), ALU.is_equal)

        def times_value(ops, g, a):
            value = rb[:, 6 + a, g * QG:(g + 1) * QG].rearrange("p (q o) -> p q o", o=1).to_broadcast([P, QG, E * HI])
            return ops.tensor_tensor(hi_vals[:, g % 2, :, a, :], one_hi[:, g % 2, :, :], value, ALU.mult)

        def residual(engine, ops, b):
            wait_apart(engine, heads_normed, at(b, 1, 1))
            wait_apart(engine, back_turned, START + at(b, 4, 0))
            wait_apart(engine, xn_stored, at(b, 16, 16))
            for t in range(ST):
                ins = ops.tensor_tensor(xn[:, t, :].rearrange("p (h c) -> p h c", h=NH), heads[b[1] % 2][:, t, :, 0:DH],
                                        gvec[:, :].rearrange("p (h c) -> p h c", h=NH), ALU.mult)
            ins.then_inc(heads_weighed, 1)
            wait_apart(engine, x_back_in, at(b, 16, 16))
            wait_apart(engine, heads_weighed, at(b, 1, 1))
            for t in range(ST):
                ins = ops.tensor_tensor(x_back[:, t, :], x_back[:, t, :], xn[:, t, :], ALU.add)
            ins.then_inc(x1_made, 1)

        def there(b):
            return not isinstance(b[0], int) or 0 <= b[1] < B

        YB, HB, XB = 0, 3, 6

        STEPS = NC * HT
        TURN_AT = {c * HT + 7 + 2 * t: CT * c + t for c in range(NC) for t in range(CT)}
        AHEAD = 2

        def turns_of(n, last):
            m = TURN_AT.get(n)
            return [] if m is None or (last and m >= HI - CT) else [m]

        def x_place(m):
            return (m // CT + 1) % NC, m % CT

        passed = sem("passed")
        from_start = [rows_free, y_taken, y_ready, x1_made, back_turned, back_copied, logits_made, logits_copied]

        def wait_past(eng, signal, value):
            if not isinstance(value, int) or value > 0:
                eng.wait_ge(signal, value)

        def wait_apart(eng, signal, value):
            if isinstance(value, int):
                return wait_past(eng, signal, value)
            eng.wait_ge(signal, value)
            eng.sem_inc(passed, 1)

        def wait_step(eng, e, n):
            c, j = divmod(n, HT)
            if j == HT - 1:
                eng.wait_ge(y_tile, e * HI + CT * (c + 1))
            else:
                eng.wait_ge(y_step, e * (NC * (HT - 1)) + (c * (HT - 1) + j + 1))

        def w_at(j):
            return HT - 1 - j

        def raw_w1(j):
            return raw[:, (j // 2) % 2, 0:2 * D].rearrange("p (k c) -> p k c", k=KT)[:, :, (j % 2) * P:(j % 2 + 1) * P]

        def raw_w2(j):
            return raw[:, (j // 2) % 2, (2 + j % 2) * D:(3 + j % 2) * D]

        block = stack.enter_context(nc.Block())

        @block.sync
        def _(sp):
            def load_front(b):
                wait_apart(sp, q_made, at(b, 4, 0))
                sp.dma_start(x_front[:, :, :], x_rows[number(b)]).then_inc(x_front_in, 16)

            def load_ctx(b):
                p = b[1] % 2
                wait_apart(sp, head_summed, at(b, 4, -4))
                for t in range(ST):
                    sp.dma_start(vs[p][:, t, :, 0:DH], ctx_rows[number(b), t]).then_inc(ctx_in_sb[p], 16)

            def load_back(b):
                wait_apart(sp, x1_stored, at(b, 16, 16))
                sp.dma_start(x_back[:, :, :], x_rows[number(b)]).then_inc(x_back_in, 16)

            def spread_negmax(b):
                p = b[1] % 2
                wait_apart(sp, negrow_made, at(b, 1, 1))
                sp.dma_start(negmax_dram[number(b)].rearrange("(h s) -> h s", h=NH), g_neg[:, :]).then_inc(negrow_out, 16)
                wait_apart(sp, negrow_out, at(b, 16, 16))
                wait_apart(sp, decay_made, at(b, 4, -4))
                sp.dma_start(negmax[p][:, :, :].rearrange("q h s -> q (h s)"),
                             negmax_dram[number(b)].partition_broadcast(P)).then_inc(negmax_in[p], 16)

            def store_x1(b):
                wait_apart(sp, x1_made, START + at(b, 1, 1))
                sp.dma_start(out_rows[number(b)], x_back[:, :, :]).then_inc(x1_stored, 16)

            def store_xn(b):
                wait_apart(sp, xn_made, at(b, 1, 1))
                sp.dma_start(xn_rows[number(b)], xn[:, :, :]).then_inc(xn_stored, 16)

            def slot(b):
                ahead, front, back = near(b, 2), near(b, 1), near(b, -1)
                if there(front):
                    load_ctx(front)
                if there(ahead):
                    load_front(ahead)
                if there(back):
                    load_back(back)
                    store_x1(back)
                if there(front):
                    spread_negmax(front)
                if there(back):
                    store_xn(back)

            slot((0, -2))
            sp.wait_ge(pool_const, 1)
            sp.dma_start(wload[0:NH, :], w_fg).then_inc(const_in, 16)
            sp.dma_start(wload[32:32 + NH, :], w_ig).then_inc(const_in, 16)
            sp.dma_start(gate_bias[0:NH, :], b_fg.rearrange("(h o) -> h o", o=1)).then_inc(const_in, 16)
            sp.dma_start(gate_bias[32:32 + NH, :], b_ig.rearrange("(h o) -> h o", o=1)).then_inc(const_in, 16)
            sp.dma_start(rload[:, :], w_router).then_inc(const_in, 16)
            sp.dma_start(bload[:, :], b1.rearrange("e (j p) -> (e j) p", p=P)).then_inc(const_in, 16)
            sp.dma_start(tanh_x[:, :], g_xattn.partition_broadcast(P)).then_inc(const_in, 16)
            sp.dma_start(tanh_f[:, :], g_ffn.partition_broadcast(P)).then_inc(const_in, 16)
            sp.dma_start(gvec[:, :], ln_w.partition_broadcast(P)).then_inc(const_in, 16)
            sp.dma_start(xn_dram[TOK:TOK + PAD, :], zeros[:, :]).then_inc(xn_stored, 16)
            sp.dma_start(out[TOK:TOK + PAD, :], zeros[:, :]).then_inc(x1_stored, 16)

            for b in range(-1, 2):
                slot((0, b))
            with sp.Fori(0, (B - 4) // 2) as i:
                slot((i, 2))
                slot((i, 3))
            for b in range(B - 2, B):
                slot((0, b))

            def load_weights(e, g, wait):
                if wait is not None:
                    wait_apart(sp, w_ready, wait)
                sp.dma_start(raw[:, g % 2, 0:2 * D].rearrange("p (k c) -> p k c", k=KT),
                             w1[e].rearrange("(k p) n -> p k n", p=P)[:, :, 2 * g * P:(2 * g + 2) * P]).then_inc(raw_in[g % 2], 16)
                sp.dma_start(raw[:, g % 2, 2 * D:4 * D].rearrange("p (j n) -> p j n", j=2),
                             w2[e, 2 * g * P:(2 * g + 2) * P, :].rearrange("(j p) n -> p j n", p=P)).then_inc(raw_in[g % 2], 16)

            load_back(LAST_BATCH)
            for g in range(HT // 2):
                if g == HT // 4:
                    store_x1(LAST_BATCH)
                    store_xn(LAST_BATCH)
                load_weights(0, g, None if g < 2 else 2 * (g - 1))

            def load_b2(e):
                wait_apart(sp, y_taken, START + e * HI)
                sp.dma_start(b2_row[:, :], b2[e].partition_broadcast(P)).then_inc(b2_in, 16)

            with sp.Fori(0, E - 1) as e:
                load_b2(e)
                for g in range(HT // 2):
                    load_weights(e + 1, g, e * HT + (HT + 2 * (g - 1)))
            load_b2(E - 1)
            sp.wait_ge(y_added, 16 * HI * E)
            sp.wait_ge(x1_stored, 16 * (B + 1))
            sp.wait_ge(xn_stored, 16 * (B + 1))
            sp.wait_ge(const_in, 16 * N_CONST)

        @block.gpsimd
        def _(pool):
            for s in from_start:
                pool.sem_inc(s, START)
            G.memset(wload[:, :], 0.0)
            G.memset(zeros[:, :], 0.0).then_inc(pool_const, 1)
            G.memset(ones[:, :], 1.0).then_inc(pool_const, 1)
            pool.wait_ge(pool_const, 2)
            G.affine_select(out=ident[:, :], in_=ones[:, 0:P], compare_op=ALU.is_equal, fill=0.0, base=0,
                            pattern=[[-1, P]], channel_multiplier=1).then_inc(pool_const, 1)
            for p in range(2):
                G.memset(vs[p][:, :, :, DH:VW], 1.0)
            G.affine_select(out=upper[:, :], in_=ones[:, 0:P], compare_op=ALU.is_gt, fill=0.0, base=0,
                            pattern=[[1, P]], channel_multiplier=-1)
            G.memset(g_rows[:, :], 0.0)
            G.iota(iota_e[:, :, :], pattern=[[0, NQ], [-1, E]], base=E, channel_multiplier=0,
                   allow_small_or_imprecise_dtypes=True)
            G.iota(iota_p[:, :], pattern=[[1, P]], base=0, channel_multiplier=0,
                   allow_small_or_imprecise_dtypes=True)
            G.iota(token[:, :].rearrange("p (k t) -> p k t", k=TOPK), pattern=[[0, TOPK], [P, TT]], base=-TOK,
                   channel_multiplier=1, allow_small_or_imprecise_dtypes=True)
            G.iota(pad_row[:, :], pattern=[[0, 1]], base=TOK, channel_multiplier=1,
                   allow_small_or_imprecise_dtypes=True).then_inc(pool_const, 1)

            def mask(b, h):
                wait_apart(pool, decay_made, at(b, 4, h + 1))
                diag = decay[h % 2][:, :, :].rearrange("p t s -> p (t s)")
                diag = bass.AP(diag.tensor, diag.offset, [list(diag.ap[0]), [S + P, ST], [1, P]])
                G.affine_select(out=diag, in_=diag, compare_op=ALU.is_ge, fill=0.0, base=0,
                                pattern=[[0, ST], [1, P]], channel_multiplier=-1).then_inc(decay_masked, 1)

            def slot(b):
                if there(b):
                    mask(b, 0)
                    mask(b, 1)
                if there(near(b, -1)):
                    residual(pool, G, near(b, -1))
                if there(b):
                    mask(b, 2)
                    mask(b, 3)

            for b in range(0, 2):
                slot((0, b))
            with pool.Fori(0, (B - 4) // 2) as i:
                slot((i, 2))
                slot((i, 3))
            for b in range(B - 2, B):
                slot((0, b))

            def first_rests(tiles):
                for j in tiles:
                    pool.wait_ge(w_upper, j + 1)
                    G.tensor_tensor(w_lo[:, w_at(j), 0:D].rearrange("p (k c) -> p k c", k=KT), raw_w1(j),
                                    w_hi[:, w_at(j), 0:D].bitcast(F32).rearrange("p (k c) -> p k c", k=KT), ALU.subtract)
                    G.tensor_tensor(w_lo[:, w_at(j), D:2 * D], raw_w2(j), w_hi[:, w_at(j), D:2 * D].bitcast(F32), ALU.subtract)\
                        .then_inc(w_ready, 1)

            first_rests(EARLY)
            first_rests(MIDDLE)
            for g in range(NQ // QG):
                pool.wait_ge(one_hi_made, g + 1)
                times_value(G, g, 0).then_inc(rows_spread, 1)

            pool.wait_ge(table_made, 2)
            pool.wait_ge(xn_stored, 16 * (B + 1))
            pool.wait_ge(x1_stored, 16 * (B + 1))
            pool.wait_ge(const_in, 16 * N_CONST)

            def gather(rows, ring, free):
                if free is not None:
                    wait_apart(pool, rows_turned, free)
                G.indirect_dma_start(out=gathered[0:RT, ring, :], out_offset=None, in_=xn_dram[:, :],
                                     in_offset=bass.IndirectOffsetOnAxis(ap=rows[0:RT, :], axis=0)
                                     ).then_inc(row_in[ring], 16)

            def add_rows(e, u, ordered=True):
                wait_apart(pool, y_ready, START + e * HI + (u + 1))
                if u > 0 and ordered:
                    wait_apart(pool, y_added, e * (16 * HI) + 16 * u)
                G.indirect_dma_start(out=out[:, :], out_offset=bass.IndirectOffsetOnAxis(ap=rows_add[u % CT][0:RT, :], axis=0),
                                     in_=y_out[0:RT, u % CT, :], in_offset=None, compute_op=ALU.add,
                                     bounds_check=TOK + PAD - 1, oob_is_err=True).then_inc(y_added, 16)

            for t in range(CT):
                gather(slot_row[:, t:t + 1], t, None)
            first_rests(LATE)

            def expert(e, last):
                turns = HI - CT if last else HI
                for ring in range(CT):
                    wait_apart(pool, row_in[ring], e * (16 * NC) + 16)
                G.tensor_copy(rows_turn[:, 0:turns], slot_row[:, bass.ds(e * HI + CT, turns)]).then_inc(turn_rows_copied, 1)
                wait_apart(pool, turn_rows_copied, e + 1)
                for c in range(NC):
                    if c < NC - 1 or not last:
                        for m in range(CT * c, CT * c + CT):
                            gather(rows_turn[:, m:m + 1], m % CT, e * HI + (m + 1))
                    for t in range(CT):
                        add_rows(e, CT * c + t, ordered=not (last and c == NC - 1 and t > 0))
                wait_apart(pool, y_added, e * (16 * HI) + 16 * HI)
                pool.sem_inc(rows_free, 1)

            with pool.Fori(0, E - 1) as e:
                expert(e, False)
            expert(E - 1, True)

        @block.tensor
        def _(pe):
            pe.wait_ge(const_in, 16 * N_CONST)
            pe.wait_ge(pool_const, 4)
            for k in range(3 * KT):
                T.transpose(PS[:, 0, k * GR:(k + 1) * GR], wload[:, k * P:(k + 1) * P], ident[0:GR, 0:GR])
            for k in range(KT):
                T.transpose(PS[:, 1, k * E:(k + 1) * E], rload[:, k * P:(k + 1) * P], ident[0:E, 0:E])
            T.transpose(PS[:, 2, 0:P], bload[:, :], ident[:, :]).then_inc(weights_turned, 1)
            pe.wait_ge(consts_ready, 1)

            def turn_front(b, pos):
                p, t = b[1] % 2, pos % ST
                if pos < ST:
                    pe.wait_ge(q_made, at(b, 4, t + 1))
                elif t == 0:
                    pe.wait_ge(ctx_in_sb[p], at_own(b, 64, 64))
                wait_past(pe, front_copied, at(b, 8, pos - 1))
                if pos == 1 and b[1] >= 3:
                    pe.wait_ge(logits_copied, START + at(b, 1, -3))
                for k in range(KT):
                    rows = qn[:, t, k * P:(k + 1) * P] if pos < ST else vs[p][:, t, k, 0:DH]
                    ins = T.transpose(PS[:, TURN + pos % 2, k * P:(k + 1) * P], rows, ident[:, :])
                ins.then_inc(front_turned, 1)

            def gate_products(b):
                p = b[1] % 2
                pe.wait_ge(front_copied, at(b, 8, 8))
                wait_past(pe, gates_taken, at(b, 1, 0))
                if b[1] >= 2:
                    pe.wait_ge(back_copied, START + at(b, 4, -8))
                for k in range(2 * KT):
                    src = qT[p][:, k, :] if k < KT else kT[p][:, k - KT, :]
                    ins = T.matmul(PS[0:GR, GATE, :], wgate[:, k, :], src, start=(k == 0), stop=(k == 2 * KT - 1))
                ins.then_inc(gates_made, 1)

            def gate_columns(b):
                wait_apart(pe, gate_rows_made, at(b, 1, 1))
                wait_apart(pe, cols_copied, at(b, 1, 0))
                for t in range(ST):
                    ins = T.transpose(cols_ps[:, t, :], g_rows[:, t * P:(t + 1) * P], ident[0:GR, 0:GR])
                ins.then_inc(cols_made, 1)

            def scores(b, h):
                p = b[1] % 2
                for place, t in enumerate(SCORE_ORDER):
                    wait_past(pe, scored, at(b, 16, 4 * h + READ[place]))
                    T.matmul(score_ps[t], kT[p][:, h, t * P:(t + 1) * P], qT[p][:, h, t * P:S],
                             start=True, stop=True).then_inc(scores_made, 1)

            def outputs(b, h):
                p = b[1] % 2
                wait_past(pe, head_copied, at(b, 4, h))
                for s in range(ST):
                    pe.wait_ge(scored, at(b, 16, 4 * h + NEEDED[s]))
                    for t in range(s + 1):
                        ins = T.matmul(head_ps[:, s, 0:DH + 1], decay[h % 2][:, t, s * P:(s + 1) * P],
                                       vs[p][:, t, h, 0:DH + 1], start=(t == 0), stop=(t == s))
                ins.then_inc(head_summed, 1)

            def columns_before(b, more):
                return min(b[1] + more, B) if isinstance(b[0], int) else at(b, 1, more)

            def turn_back(b, t, spread):
                pe.wait_ge(xn_made, at(b, 1, 1))
                if t == 0:
                    pe.wait_ge(cols_copied, columns_before(b, 3))
                if t == 0 or not spread:
                    pe.wait_ge(back_copied, START + at(b, 4, t))
                for k in range(KT):
                    ins = T.transpose(back_ps(t, spread)[:, k * P:(k + 1) * P], xn[:, t, k * P:(k + 1) * P], ident[:, :])
                ins.then_inc(back_turned, 1)

            def router_products(b):
                pe.wait_ge(back_copied, START + at(b, 4, 4))
                pe.wait_ge(front_copied, min(b[1] + 4, B) * 8 if isinstance(b[0], int) else at(b, 8, 32))
                pe.wait_ge(logits_copied, START + at(b, 1, 0))
                for k in range(KT):
                    ins = T.matmul(PS[0:E, TURN + 1, :], wrouter[:, k, :], xnT[:, k, :], start=(k == 0), stop=(k == KT - 1))
                ins.then_inc(router_summed, 1)

            def turn_logits(b):
                wait_apart(pe, router_copied, at(b, 1, 1))
                for t in range(ST):
                    ins = T.transpose(logit_ps[:, t, :], logit_rows[:, t * P:(t + 1) * P], ident[0:E, 0:E])
                ins.then_inc(logits_made, 1)

            def slot(b):
                front, last = near(b, 1), near(b, -2)

                def turns(kind, *positions):
                    for t in positions:
                        if kind == "q" and there(front):
                            turn_front(front, t)
                        if kind == "ctx" and there(front):
                            turn_front(front, ST + t)
                        if kind == "x1" and there(last):
                            turn_back(last, t, not there(b))

                turns("q", 0, 1)
                turns("x1", 0)
                turns("q", 2)
                turns("x1", 1)
                turns("q", 3)
                turns("x1", 2)
                if there(b):
                    scores(b, 1)
                turns("x1", 3)
                if there(last) and not there(b):
                    router_products(last)
                    turn_logits(last)
                if there(b):
                    outputs(b, 0)
                turns("ctx", 0, 1, 2, 3)
                if there(front):
                    gate_products(front)
                if there(b):
                    scores(b, 2)
                    outputs(b, 1)
                if there(last) and there(b):
                    router_products(last)
                if there(b):
                    scores(b, 3)
                    outputs(b, 2)
                if there(last) and there(b):
                    turn_logits(last)
                if there(front):
                    gate_columns(front)
                if there(b):
                    outputs(b, 3)
                if there(front):
                    scores(front, 0)

            for b in range(-2, 2):
                slot((0, b))
            with pe.Fori(0, (B - 4) // 2) as i:
                slot((i, 2))
                slot((i, 3))
            for b in range(B - 2, B + 2):
                slot((0, b))

            pe.wait_ge(choice_made, 1)
            flat = chosen[:, :, :].rearrange("p q e -> p (q e)")
            T.matmul(PS[:, 0, :], upper[:, :], flat, start=True, stop=True)
            T.matmul(PS[:, 1, :], ones[:, 0:P], flat, start=True, stop=True).then_inc(ranks_made, 1)
            for q in range(NQ):
                if q % QG == 0:
                    pe.wait_ge(onehot_made, q // QG + 1)
                    pe.wait_ge(rows_spread, q // QG + 1)
                T.matmul(PS[:, 2, 0:2 * E * HI], one_lo[:, q // QG % 2, q % QG, :], hi_vals[:, q // QG % 2, q % QG, :, :].rearrange("p a h -> p (a h)"),
                         start=(q == 0), stop=(q == NQ - 1)).then_inc(onehot_used, 1)

            def turn_rows(t, bank, landed, copied):
                wait_apart(pe, row_in[t], landed)
                if copied is not None:
                    wait_apart(pe, x_ready, copied)
                for k in range(KT):
                    ins = T.transpose(PS[:, XB + bank, k * P:k * P + RT], gathered[0:RT, t, k * P:(k + 1) * P], ident[0:RT, 0:RT])
                ins.then_inc(rows_turned, 1)

            pe.wait_ge(table_made, 2)
            for t in range(CT):
                turn_rows(t, t % 2, 16, None if t < 2 else t - 1)

            def first_layer(e, n):
                c, j = n // HT % NC, n % HT
                if j == 0:
                    pe.wait_ge(x_ready, e * HI + CT * (n // HT + 1))
                if n // HT % NC == 0:
                    pe.wait_ge(w_ready, e * HT + (n // STEPS * HT + j + 1))
                if n >= 3:
                    pe.wait_ge(h_upper, e * STEPS + (n - 2))
                for k in range(KT):
                    for a, (w, v) in enumerate(((w_hi, x_hi), (w_hi, x_lo), (w_lo, x_hi))):
                        ins = T.matmul(PS[:, HB + n % 3, 0:CW], w[:, w_at(j), k * P:(k + 1) * P], v[:, c, k, :],
                                       start=(k == 0 and a == 0), stop=(k == KT - 1 and a == 2))
                ins.then_inc(h_summed, 1)

            def expert(e, last):
                def second_layer(n):
                    c, j = divmod(n, HT)
                    pe.wait_ge(h_split, e * STEPS + (n + 1))
                    for t in range(CT):
                        if j == 0:
                            pe.wait_ge(y_taken, START + e * HI + (CT * (c - 1) + t + 1))
                        for a, (h, w) in enumerate(((h_hi, w_hi), (h_hi, w_lo), (h_lo, w_hi))):
                            ins = T.matmul(PS[0:RT, YB + t, :], h[:, n % 3, t * RT:(t + 1) * RT], w[:, w_at(j), D:2 * D],
                                           start=(j == 0 and a == 0), stop=(j == HT - 1 and a == 2))
                        if j == HT - 1:
                            ins.then_inc(y_tile, 1)
                    if j < HT - 1:
                        ins.then_inc(y_step, 1)

                for n in range(STEPS):
                    if n + AHEAD < STEPS or not last:
                        first_layer(e, n + AHEAD)
                    for m in turns_of(n, last):
                        turn_rows(m % CT, (m + 1) % 2, e * (16 * NC) + 16 * (m // CT + 2), e * HI + (m + 2))
                    second_layer(n)

            for n in range(AHEAD):
                first_layer(0, n)
            with pe.Fori(0, E - 1) as e:
                expert(e, False)
            expert(E - 1, True)

        @block.scalar
        def _(act):
            def seed(kind, b, chain):
                n = (ST, ST * NH, ST)[kind]
                act.wait_ge(var_made[kind], at(b, 1, 1))
                chain(A.activation(small[kind][:, 3, 0:n], small[kind][:, 2, 0:n], ACT.Ln))
                A.activation(small[kind][:, 3, 0:n], small[kind][:, 3, 0:n], ACT.Exp, scale=-0.5).then_inc(seed_made[kind], 1)

            def copy_front(b, pos):
                dst = (qT, kT)[pos // ST][b[1] % 2][:, :, (pos % ST) * P:(pos % ST + 1) * P]
                act.wait_ge(front_turned, at(b, 8, pos + 1))
                if pos == 0:
                    wait_past(act, head_summed, at(b, 4, -4))
                A.copy(dst, PS[:, TURN + pos % 2, :].rearrange("p (k c) -> p k c", k=KT)).then_inc(front_copied, 1)

            def softplus(b, chain):
                act.wait_ge(abs_made, at(b, 1, 1))
                chain(A.activation(g_t[:, :], g_t[:, :], ACT.Exp, scale=-1.0))
                A.activation(g_t[:, :], g_t[:, :], ACT.Ln, bias=1.0).then_inc(softplus_made, 1)

            def exp_negmax(b):
                act.wait_ge(cols_copied, at(b, 1, 1))
                wait_past(act, x1_made, START + at(b, 1, -1))
                A.activation(expneg[b[1] % 2][:, :, :], cols[b[1] % 2][:, :, 32:32 + NH], ACT.Exp).then_inc(expneg_made, 1)

            def exponentials(b, h):
                p = b[1] % 2
                if h == 0:
                    act.wait_ge(cols_copied, at(b, 1, 1))
                    act.wait_ge(negmax_in[p], at_own(b, 16, 16))
                wait_past(act, head_summed, at(b, 4, h - 1))
                for t in range(ST):
                    ins = A.activation(decay[h % 2][:, t, t * P:S], negmax[p][:, h, t * P:S], ACT.Exp,
                                       bias=cols[p][:, t, h:h + 1])
                ins.then_inc(decay_made, 1)

            def copy_head(b, h):
                act.wait_ge(head_summed, at(b, 4, h + 1))
                A.copy(heads[b[1] % 2][:, :, h, 0:DH + 1], head_ps[:, :, 0:DH + 1]).then_inc(head_copied, 1)

            def copy_back(b, t, spread):
                act.wait_ge(back_turned, START + at(b, 4, t + 1))
                if t == 0:
                    act.wait_ge(logits_made, START + at(b, 1, 0))
                A.copy(xnT[:, :, t * P:(t + 1) * P], back_ps(t, spread).rearrange("p (k c) -> p k c", k=KT)).then_inc(back_copied, 1)

            def copy_router(b):
                act.wait_ge(router_summed, at(b, 1, 1))
                act.wait_ge(logits_made, START + at(b, 1, 0))
                A.copy(logit_rows[:, :], PS[0:E, TURN + 1, :]).then_inc(router_copied, 1)

            def slot(b, chain):
                ahead, front, back, last = near(b, 2), near(b, 1), near(b, -1), near(b, -2)

                def copies(kind, *positions):
                    for t in positions:
                        if kind == "q" and there(front):
                            copy_front(front, t)
                        if kind == "ctx" and there(front):
                            copy_front(front, ST + t)
                        if kind == "x1" and there(last):
                            copy_back(last, t, not there(b))

                copies("q", 0, 1)
                copies("x1", 0)
                copies("q", 2)
                copies("x1", 1)
                copies("q", 3)
                if there(back):
                    seed(1, back, chain)
                if there(b):
                    exponentials(b, 1)
                copies("x1", 2, 3)
                if there(b):
                    copy_head(b, 0)
                copies("ctx", 0, 1, 2, 3)
                if there(b):
                    exponentials(b, 2)
                    exp_negmax(b)
                if there(ahead):
                    seed(0, ahead, chain)
                if there(front):
                    softplus(front, chain)
                if there(b):
                    copy_head(b, 1)
                    exponentials(b, 3)
                if there(last):
                    copy_router(last)
                if there(back):
                    seed(2, back, chain)
                if there(b):
                    copy_head(b, 2)
                    copy_head(b, 3)
                if there(front):
                    exponentials(front, 0)

            fixed = Chain(act, a_setup)
            A.preload_act_table_set("natural_log_exp_and_others")
            slot((0, -2), fixed)
            act.wait_ge(const_in, 16 * N_CONST)
            A.activation(tanh_x[:, :], tanh_x[:, :], ACT.Tanh)
            A.activation(tanh_f[:, :], tanh_f[:, :], ACT.Tanh).then_inc(tanh_made, 1)
            A.preload_act_table_set("natural_log_exp_and_others")
            for b in range(-1, 2):
                slot((0, b), fixed)
            with act.Fori(0, (B - 4) // 2) as i:
                chain = Chain(act, a_chain, i, 8)
                slot((i, 2), chain)
                slot((i, 3), chain)
                chain.closed()
            for b in range(B - 2, B):
                slot((0, b), fixed)

            def upper_x(c, t, bank, turned):
                act.wait_ge(rows_turned, turned)
                A.copy(x_hi[:, c, :, t * RT:(t + 1) * RT],
                       PS[:, XB + bank, :].rearrange("p (k c) -> p k c", k=KT)[:, :, 0:RT]).then_inc(x_upper, 1)

            def upper_w(j, raw_arrived, free=None):
                g, jj = j // 2, j % 2
                if jj == 0:
                    act.wait_ge(raw_in[g % 2], raw_arrived)
                if free is not None:
                    wait_step(act, *free)
                A.copy(w_hi[:, w_at(j), 0:D].rearrange("p (k c) -> p k c", k=KT), raw_w1(j))
                A.copy(w_hi[:, w_at(j), D:2 * D], raw_w2(j)).then_inc(w_upper, 1)

            def first_w(tiles):
                for j in tiles:
                    upper_w(j, 32 * (j // 4 + 1))

            act.wait_ge(head_summed, NH * B)
            for t in range(ST):
                copy_back(near(LAST_BATCH, -1), t, True)
            seed(1, LAST_BATCH, fixed)
            copy_router(near(LAST_BATCH, -1))
            first_w(EARLY[:4])
            seed(2, LAST_BATCH, fixed)
            for t in range(ST):
                copy_back(LAST_BATCH, t, True)
            first_w(EARLY[4:6])
            copy_router(LAST_BATCH)
            act.wait_ge(b_sub, 1)
            A.activation(prob[:, :, :], prob[:, :, :], ACT.Exp).then_inc(b_exp, 1)
            first_w(EARLY[6:])
            act.wait_ge(x1_stored, 16 * (B + 1))
            act.wait_ge(xn_stored, 16 * (B + 1))
            act.wait_ge(logits_copied, START + B)
            first_w(MIDDLE)
            first_w(LATE)

            act.wait_ge(table_made, 2)
            for t in range(CT):
                upper_x(0, t, t % 2, t + 1)

            def hidden(e, n):
                if n % STEPS == 0:
                    if n > 0:
                        act.wait_ge(h_upper, e * STEPS + n)
                    A.copy(b1_now[:, :], b1_all[:, bass.ds(e * HT + n // STEPS * HT, HT)]).then_inc(b1_copied, 1)
                    act.wait_ge(b1_copied, e + (n // STEPS + 1))
                act.wait_ge(h_summed, e * STEPS + (n + 1))
                if n >= 3:
                    act.wait_ge(h_split, e * STEPS + (n - 2))
                A.activation(h_raw[:, n % 3, :], PS[:, HB + n % 3, 0:CW], ACT.Gelu, bias=b1_now[:, n % HT:n % HT + 1])
                A.activation(h_hi[:, n % 3, :], PS[:, HB + n % 3, 0:CW], ACT.Gelu,
                             bias=b1_now[:, n % HT:n % HT + 1]).then_inc(h_upper, 1)

            def expert(e, last):
                def next_w(j):
                    upper_w(j, e * 128 + (128 + 32 * (j // 4 + 1)), (e, STEPS - HT + j))

                for n in range(AHEAD, STEPS if last else STEPS + AHEAD):
                    hidden(e, n)
                    for m in turns_of(n - AHEAD, last):
                        upper_x(*x_place(m), (m + 1) % 2, e * HI + (CT + m + 1))
                    if not last and n >= STEPS - HT + 3:
                        next_w(n - (STEPS - HT + 3))
                if not last:
                    next_w(HT - 1)

            for n in range(AHEAD):
                hidden(0, n)
            with act.Fori(0, E - 1) as e:
                expert(e, False)
            expert(E - 1, True)

        @block.vector
        def _(dve):
            link = Chain(dve, v_setup)
            V_SLOT = 29

            def newton(kind, b, n, chain):
                v, y, w = (small[kind][:, k, 0:n] for k in (2, 3, 4))
                dve.wait_ge(seed_made[kind], at(b, 1, 1))
                chain(V.tensor_tensor(w, y, v, ALU.mult))
                chain(V.tensor_tensor(w, w, y, ALU.mult))
                chain(V.tensor_scalar(w, w, -0.5, 1.5, ALU.mult, ALU.add))
                chain(V.tensor_tensor(y, y, w, ALU.mult))

            def row_stats(kind, src, chain):
                for t in range(ST):
                    ins = V.bn_stats(stats[kind][:, t, :], src[:, t, :])
                chain(ins)
                dve.sem_inc(passed, 1)
                mv = small[kind][:, 0:2, 0:ST].rearrange("p a t -> p t a")
                for t in range(ST):
                    ins = V.bn_aggr(mv[:, t, :], stats[kind][:, t, :])
                chain(ins)
                V.tensor_scalar(small[kind][:, 2, 0:ST], small[kind][:, 1, 0:ST], LN_EPS, None, ALU.add).then_inc(var_made[kind], 1)

            def normalise(kind, t, dst, src):
                return V.tensor_scalar(dst[:, t, :], src[:, t, :], small[kind][:, 0, t:t + 1], small[kind][:, 3, t:t + 1],
                                       ALU.subtract, ALU.mult)

            def front_stats(b, chain):
                dve.wait_ge(x_front_in, at(b, 16, 16))
                row_stats(0, x_front, chain)

            def front_norm(b, chain):
                newton(0, b, ST, chain)
                wait_past(dve, front_turned, at(b, 8, -4))
                for t in range(ST):
                    normalise(0, t, qn, x_front).then_inc(q_made, 1)

            def gates_first(b, chain):
                dve.wait_ge(gates_made, at(b, 1, 1))
                gates = PS[:, GATE, :]
                V.tensor_scalar(g_f[:, :], gates[0:NH, :], gate_bias[0:NH, 0:1], None, ALU.add)
                chain(V.tensor_scalar(g_i[:, :], gates[32:32 + NH, :], gate_bias[32:32 + NH, 0:1], None, ALU.add))
                dve.sem_inc(gates_taken, 1)
                V.scalar_tensor_tensor(g_t[:, :], g_f[:, :], -1.0, g_f[:, :], ALU.mult, ALU.max).then_inc(abs_made, 1)

            def gates_second(b, chain):
                dve.wait_ge(softplus_made, at(b, 1, 1))
                chain(V.scalar_tensor_tensor(g_f[:, :], g_f[:, :], 0.0, g_t[:, :], ALU.min, ALU.subtract))
                chain(V.tensor_tensor_scan(g_cum[:, :], ones[0:NH, :], g_f[:, :], 0.0, ALU.mult, ALU.add))
                chain(V.tensor_tensor(g_i[:, :], g_i[:, :], g_cum[:, :], ALU.subtract))
                chain(V.tensor_tensor_scan(g_max[:, :], ones[0:NH, :], g_i[:, :], LOWEST, ALU.mult, ALU.max))
                wait_past(dve, negrow_out, at(b, 16, 0))
                wait_past(dve, cols_made, at(b, 1, 0))
                V.tensor_scalar(g_neg[:, :], g_max[:, :], -1.0, None, ALU.mult).then_inc(negrow_made, 1)
                V.tensor_copy(g_rows[0:NH, :], g_i[:, :])
                V.scalar_tensor_tensor(g_rows[32:32 + NH, :], g_cum[:, :], -1.0, g_max[:, :], ALU.mult, ALU.subtract)\
                    .then_inc(gate_rows_made, 1)

            def gate_columns(b):
                dve.wait_ge(cols_made, at(b, 1, 1))
                wait_past(dve, decay_made, at(b, 4, -4))
                wait_past(dve, expneg_made, at(b, 1, -1))
                V.tensor_copy(cols[b[1] % 2][:, :, :], cols_ps).then_inc(cols_copied, 1)

            def weigh(b, h):
                dve.wait_ge(decay_masked, at(b, 4, h + 1))
                for place, t in enumerate(SCORE_ORDER):
                    dve.wait_ge(scores_made, at(b, 16, 4 * h + MADE[place]))
                    d = decay[h % 2][:, t, t * P:S]
                    V.scalar_tensor_tensor(d, score_ps[t], SCORE_SCALE, d, ALU.mult, ALU.mult).then_inc(scored, 1)

            NHT = ST * NH

            def head_plane(k):
                return small[1][:, k, :]

            def back_stats(b, chain):
                hs, st = heads[b[1] % 2], stats[1]
                dve.wait_ge(head_copied, at(b, 4, 4))
                for t in range(ST):
                    for h in range(NH):
                        ins = V.bn_stats(st[:, t * NH + h, :], hs[:, t, h, 0:DH])
                chain(ins)
                dve.wait_ge(expneg_made, at(b, 1, 1))
                sums = hs[:, :, :, DH]
                r = head_plane(5).rearrange("p (t h) -> p t h", t=ST)
                V.scalar_tensor_tensor(r, sums, -1.0, sums, ALU.mult, ALU.max)
                V.tensor_tensor(head_plane(6), st[:, :, 1], st[:, :, 4], ALU.add)
                V.tensor_tensor(head_plane(7), st[:, :, 1], st[:, :, 4], ALU.subtract)
                chain(V.tensor_tensor(head_plane(8), st[:, :, 2], st[:, :, 5], ALU.add))
                V.tensor_tensor(r, r, expneg[b[1] % 2][:, :, :], ALU.max)
                V.tensor_scalar(head_plane(6), head_plane(6), 0.5, None, ALU.mult)
                chain(V.scalar_tensor_tensor(head_plane(7), head_plane(7), 0.25, head_plane(7), ALU.mult, ALU.mult))
                V.tensor_scalar(head_plane(5), head_plane(5), NORM_EPS, None, ALU.add)
                chain(V.scalar_tensor_tensor(head_plane(7), head_plane(8), 1.0 / DH, head_plane(7), ALU.mult, ALU.add))
                chain(V.reciprocal(head_plane(5), head_plane(5)))
                chain(V.tensor_tensor(head_plane(7), head_plane(7), head_plane(5), ALU.mult))
                chain(V.tensor_tensor(head_plane(7), head_plane(7), head_plane(5), ALU.mult))
                V.tensor_scalar(head_plane(2), head_plane(7), LN_EPS, None, ALU.add).then_inc(var_made[1], 1)

            def back_norm(b, chain):
                hs = heads[b[1] % 2]
                newton(1, b, NHT, chain)
                chain(V.tensor_tensor(head_plane(9), head_plane(3), head_plane(5), ALU.mult))
                for t in range(ST):
                    for h in range(NH):
                        k = t * NH + h
                        ins = V.tensor_scalar(hs[:, t, h, 0:DH], hs[:, t, h, 0:DH], small[1][:, 6, k:k + 1], small[1][:, 9, k:k + 1],
                                              ALU.subtract, ALU.mult)
                ins.then_inc(heads_normed, 1)

            def second_stats(b, chain):
                dve.wait_ge(x1_made, START + at(b, 1, 1))
                row_stats(2, x_back, chain)

            def second_norm(b, chain):
                newton(2, b, ST, chain)
                for t in range(ST):
                    ins = normalise(2, t, xn, x_back)
                ins.then_inc(xn_made, 1)

            def copy_logits(b):
                dve.wait_ge(logits_made, START + at(b, 1, 1))
                V.tensor_copy(logits[:, bass.ds(b[0] * 8 + 4 * b[1], ST), :] if not isinstance(b[0], int)
                              else logits[:, 4 * b[1]:4 * b[1] + ST, :], logit_ps).then_inc(logits_copied, 1)

            def slot(b, chain):
                ahead, front, back, last = near(b, 2), near(b, 1), near(b, -1), near(b, -2)
                if there(back):
                    back_stats(back, chain)
                if there(b):
                    weigh(b, 0)
                if there(back):
                    back_norm(back, chain)
                if there(b):
                    weigh(b, 1)
                if there(ahead):
                    front_stats(ahead, chain)
                    front_norm(ahead, chain)
                if there(front):
                    gates_first(front, chain)
                if there(b):
                    weigh(b, 2)
                if there(front):
                    gates_second(front, chain)
                if there(back):
                    second_stats(back, chain)
                if there(b):
                    weigh(b, 3)
                if there(front):
                    gate_columns(front)
                if there(back):
                    second_norm(back, chain)
                if there(last):
                    copy_logits(last)

            slot((0, -2), link)
            dve.wait_ge(weights_turned, 1)
            wt = PS[:, 0, 0:3 * KT * GR].rearrange("p (k g) -> p k g", g=GR)
            link(V.tensor_copy(wgate[:, :, :], wt[:, 0:2 * KT, :]))
            link(V.tensor_tensor(wgate[:, KT:2 * KT, :], wgate[:, KT:2 * KT, :], wt[:, 2 * KT:3 * KT, :], ALU.add))
            link(V.tensor_copy(wrouter[:, :, :], PS[:, 1, 0:KT * E].rearrange("p (k e) -> p k e", e=E)))
            link(V.tensor_copy(b1_all[:, :], PS[:, 2, 0:P]))
            dve.wait_ge(tanh_made, 1)
            link(V.tensor_scalar(gvec[:, :], gvec[:, :], 1.0, tanh_x[:, 0:1], ALU.add, ALU.mult))
            dve.sem_inc(consts_ready, 1)
            dve.wait_ge(consts_ready, 1)

            for b in range(-1, 2):
                slot((0, b), link)
            with dve.Fori(0, (B - 4) // 2) as i:
                chain = Chain(dve, v_chain, i, 2 * V_SLOT)
                slot((i, 2), chain)
                slot((i, 3), chain)
                chain.closed()
            for b in range(B - 2, B):
                slot((0, b), link)
            back_stats(LAST_BATCH, link)
            back_norm(LAST_BATCH, link)
            residual(dve, V, LAST_BATCH)
            copy_logits(near(LAST_BATCH, -1))
            second_stats(LAST_BATCH, link)
            second_norm(LAST_BATCH, link)
            copy_logits(LAST_BATCH)

            link = Chain(dve, b_chain)
            top = rb[:, 0, :]
            dve.wait_ge(logits_copied, START + B)

            def over_e(v, n):
                return v.rearrange("p (q o) -> p q o", o=1).to_broadcast([P, n, E])

            link(V.tensor_reduce(rb[:, 1, 0:TT], logits[:, :, :], AX.X, ALU.max))
            V.tensor_tensor(prob[:, :, :], logits[:, :, :], over_e(rb[:, 1, 0:TT], TT), ALU.subtract).then_inc(b_sub, 1)
            dve.wait_ge(b_exp, 1)
            link(V.tensor_reduce(rb[:, 1, 0:TT], prob[:, :, :], AX.X, ALU.add))
            link(V.reciprocal(rb[:, 1, 0:TT], rb[:, 1, 0:TT]))
            link(V.tensor_tensor(prob[:, :, :], prob[:, :, :], over_e(rb[:, 1, 0:TT], TT), ALU.mult))
            for k in range(TOPK):
                q0, q1 = k * TT, (k + 1) * TT
                first = iota_e[:, q0:q1, :]
                link(V.tensor_reduce(top[:, q0:q1], prob[:, :, :], AX.X, ALU.max))
                link(V.tensor_tensor(work[:, q0:q1, :], prob[:, :, :], over_e(top[:, q0:q1], TT), ALU.is_equal))
                link(V.tensor_tensor(work[:, q0:q1, :], work[:, q0:q1, :], first, ALU.mult))
                link(V.tensor_reduce(rb[:, 2, q0:q1], work[:, q0:q1, :], AX.X, ALU.max))
                link(V.tensor_tensor(chosen[:, q0:q1, :], first, over_e(rb[:, 2, q0:q1], TT), ALU.is_equal))
                if k == 0:
                    link(V.scalar_tensor_tensor(prob[:, :, :], chosen[:, q0:q1, :], -2.0, prob[:, :, :], ALU.mult, ALU.add))
            dve.sem_inc(choice_made, 1)
            dve.wait_ge(ranks_made, 1)
            link(V.tensor_copy(work[:, :, :], PS[:, 1, :].rearrange("p (q e) -> p q e", e=E)))
            for ex in range(E):
                ins = V.tensor_tensor_scan(base[:, :, ex], ones[:, 0:NQ], work[:, :, ex], 0.0, ALU.mult, ALU.add)
            link(ins)
            link(V.tensor_tensor(base[:, :, :], base[:, :, :], work[:, :, :], ALU.subtract))
            link(V.tensor_tensor(base[:, :, :], base[:, :, :], PS[:, 0, :].rearrange("p (q e) -> p q e", e=E), ALU.add))
            link(V.tensor_tensor(base[:, :, :], base[:, :, :], chosen[:, :, :], ALU.mult))
            link(V.tensor_reduce(rb[:, 3, :], base[:, :, :], AX.X, ALU.add))
            link(V.tensor_scalar(rb[:, 4, :], rb[:, 3, :], 1.0 / RT, 0.5 / RT - 0.5, ALU.mult, ALU.add))
            link(V.tensor_scalar(rb[:, 4, :], rb[:, 4, :], ROUND, None, ALU.add))
            link(V.tensor_scalar(rb[:, 4, :], rb[:, 4, :], -ROUND, None, ALU.add))
            link(V.scalar_tensor_tensor(rb[:, 5, :], rb[:, 4, :], -float(RT), rb[:, 3, :], ALU.mult, ALU.add))
            link(V.tensor_scalar(rb[:, 2, :], rb[:, 2, :], -float(HI), float(E * HI), ALU.mult, ALU.add))
            link(V.tensor_tensor(rb[:, 4, :], rb[:, 4, :], rb[:, 2, :], ALU.add))
            link(V.tensor_scalar(rb[:, 3, :], rb[:, 3, :], float(CAP), DROPPED, ALU.is_ge, ALU.mult))
            link(V.tensor_tensor(rb[:, 4, :], rb[:, 4, :], rb[:, 3, :], ALU.add))
            V.tensor_tensor(rb[:, 6, :], token[:, :], rb[:, 5, :], ALU.subtract)
            link(V.tensor_scalar(rb[:, 7, :], top, tanh_f[:, 0:1], None, ALU.mult))
            for g in range(NQ // QG):
                if g >= 2:
                    dve.wait_ge(onehot_used, (g - 1) * QG)
                one_hot(one_hi[:, g % 2, :, :], E * HI, rb[:, 4, g * QG:(g + 1) * QG]).then_inc(one_hi_made, 1)
                one_hot(one_lo[:, g % 2, :, :], P, rb[:, 5, g * QG:(g + 1) * QG])
                dve.wait_ge(one_hi_made, g + 1)
                times_value(V, g, 1).then_inc(onehot_made, 1)
            dve.wait_ge(onehot_used, NQ)
            link(V.tensor_scalar(row_f[:, :], PS[:, 2, 0:E * HI], pad_row[:, 0:1], None, ALU.add))
            V.tensor_copy(slot_row[:, :], row_f[:, :]).then_inc(table_made, 1)
            V.tensor_copy(slot_weight[:, :], PS[:, 2, E * HI:2 * E * HI]).then_inc(table_made, 1)
            dve.wait_ge(table_made, 2)

            def rest_of_w(j, count):
                dve.wait_ge(w_upper, count)
                V.tensor_tensor(w_lo[:, w_at(j), 0:D].rearrange("p (k c) -> p k c", k=KT), raw_w1(j),
                                w_hi[:, w_at(j), 0:D].bitcast(F32).rearrange("p (k c) -> p k c", k=KT), ALU.subtract)
                V.tensor_tensor(w_lo[:, w_at(j), D:2 * D], raw_w2(j), w_hi[:, w_at(j), D:2 * D].bitcast(F32), ALU.subtract)\
                    .then_inc(w_ready, 1)

            def rest_of_x(c, t, bank, count):
                dve.wait_ge(x_upper, count)
                V.tensor_tensor(x_lo[:, c, :, t * RT:(t + 1) * RT], PS[:, XB + bank, :].rearrange("p (k c) -> p k c", k=KT)[:, :, 0:RT],
                                x_hi[:, c, :, t * RT:(t + 1) * RT].bitcast(F32), ALU.subtract).then_inc(x_ready, 1)

            dve.wait_ge(x1_stored, 16 * (B + 1))
            dve.wait_ge(xn_stored, 16 * (B + 1))
            for t in range(CT):
                rest_of_x(0, t, t % 2, t + 1)

            def split_hidden(e, n):
                dve.wait_ge(h_upper, e * STEPS + (n + 1))
                V.tensor_tensor(h_lo[:, n % 3, :], h_raw[:, n % 3, :], h_hi[:, n % 3, :].bitcast(F32), ALU.subtract)\
                    .then_inc(h_split, 1)

            def expert(e, last):
                dve.wait_ge(y_ready, START + e * HI)
                V.tensor_copy(weight_now[:, :], slot_weight[:, bass.ds(e * HI, HI)]).then_inc(weight_copied, 1)
                dve.wait_ge(weight_copied, e + 1)

                def take(c):
                    for t in range(CT):
                        u = CT * c + t
                        dve.wait_ge(y_tile, e * HI + (u + 1))
                        if u == 0:
                            dve.wait_ge(b2_in, e * 16 + 16)
                        if c == 0:
                            dve.wait_ge(rows_free, START + e)
                        else:
                            dve.wait_ge(y_added, e * (16 * HI) + 16 * (u - CT + 1))
                        V.tensor_tensor(y_out[0:RT, t, :], PS[0:RT, YB + t, :], b2_row[0:RT, :], ALU.add).then_inc(y_taken, 1)

                def weigh_rows(c):
                    for t in range(CT):
                        u = CT * c + t
                        V.tensor_copy(rows_add[t][:, :], slot_row[:, bass.ds(e * HI + u, 1)])
                        dve.wait_ge(y_taken, START + e * HI + (u + 1))
                        V.tensor_scalar(y_out[0:RT, t, :], y_out[0:RT, t, :], weight_now[0:RT, u:u + 1], None,
                                        ALU.mult).then_inc(y_ready, 1)

                def next_w(j):
                    rest_of_w(j, e * HT + (HT + j + 1))

                for n in range(AHEAD, STEPS if last else STEPS + AHEAD):
                    split_hidden(e, n)
                    for m in turns_of(n - AHEAD, last):
                        rest_of_x(*x_place(m), (m + 1) % 2, e * HI + (CT + m + 1))
                    if n > HT and n % HT == AHEAD - 1:
                        take(n // HT - 1)
                    if not last and n >= STEPS - HT + 3:
                        next_w(n - (STEPS - HT + 3))
                    if n > HT and n % HT == AHEAD - 1:
                        weigh_rows(n // HT - 1)
                    if n > STEPS:
                        next_w(HT - 1)
                if last:
                    take(NC - 1)
                    weigh_rows(NC - 1)

            for n in range(AHEAD):
                split_hidden(0, n)
            with dve.Fori(0, E - 1) as e:
                expert(e, False)
            expert(E - 1, True)


_INS = ['x', 'ctx_1024', 'g_xattn', 'g_ffn', 'L0_xattn_w_igate', 'L0_xattn_b_igate', 'L0_xattn_w_fgate',
        'L0_xattn_b_fgate', 'L0_xattn_ln_weight', 'L0_ffn_Wg', 'L0_ffn_W1', 'L0_ffn_b1', 'L0_ffn_W2', 'L0_ffn_b2']


def kernel(**inputs):
    import numpy as _np
    import concourse.bacc as _bacc
    from concourse import mybir as _mybir
    from concourse.bass_utils import run_bass_kernel_spmd as _run

    nc = _bacc.Bacc("TRN2", target_bir_lowering=False, num_devices=1)
    arrays, args = {}, []
    for name in _INS:
        a = _np.ascontiguousarray(inputs[name])
        arrays[f"in_{name}_dram"] = a
        args.append(nc.dram_tensor(f"in_{name}_dram", a.shape, _mybir.dt.from_np(a.dtype), kind="ExternalInput").ap())
    args.append(nc.dram_tensor("out_0_dram", (TOK + PAD, D), _mybir.dt.float32, kind="ExternalOutput").ap())
    build(nc, *args)
    r = _run(nc, [arrays], core_ids=[0])
    return r.results[0]["out_0_dram"][0:TOK].reshape(B, S, D)
```
